# Optimizing a Trainium2 kernel written in Bass

```python
import numpy as np
import jax
import jax.numpy as jnp

def _softmax(x, axis=-1):
    return jax.nn.softmax(x, axis=axis)

def _gelu(x):
    return jax.nn.gelu(x, approximate=True)

def _silu(x):
    return jax.nn.silu(x)

def _sigmoid(x):
    return jax.nn.sigmoid(x)

def _layernorm(x, axis=-1, eps=1e-05):
    m = jnp.mean(x, axis=axis, keepdims=True)
    v = jnp.var(x, axis=axis, keepdims=True)
    return (x - m) / jnp.sqrt(v + eps)

def _scatter_add(tgt, idx, src, axis=0):
    return tgt.at[idx].add(src)

def _segment_sum(src, seg, n):
    return jax.ops.segment_sum(src, seg, n)
kernel_name = 'mk_recurrent_d1_jaxref_r2_e02a45'

def setup_inputs(seed: int=0):
    np.random.seed(seed)
    _w = jnp.asarray

    def _L0_attn_setup():
        import jax, jax.numpy as jnp
        import numpy as np
        TTT_LR = 0.01
        LN_EPS = 1e-05
        key = jax.random.key(seed)
        ks = jax.random.split(key, 4)
        B, S, D, DS = (4, 1024, 512, 64)
        sc = 1.0 / np.sqrt(D).astype(np.float32)
        return {'x': jax.random.normal(ks[0], (B, S, D), dtype=jnp.float32), 'Wk': jax.random.normal(ks[1], (DS, D), dtype=jnp.float32) * sc, 'bk': jnp.zeros((DS,), jnp.float32), 'Wv': jax.random.normal(ks[2], (D, D), dtype=jnp.float32) * sc, 'bv': jnp.zeros((D,), jnp.float32), 'Wq': jax.random.normal(ks[3], (DS, D), dtype=jnp.float32) * sc, 'bq': jnp.zeros((DS,), jnp.float32), 'gamma': jnp.ones((D,), jnp.float32), 'beta': jnp.zeros((D,), jnp.float32)}
    _L0_attn_in = _L0_attn_setup()

    def _L0_ffn_setup():
        import jax, jax.numpy as jnp
        import numpy as np
        DIM = 512

        def _reference_tuple_inner(x, W_r, W_k, W_v, mu_r, mu_k):
            B, T, C = x.shape
            x_prev = jnp.concatenate([jnp.zeros((B, 1, C), x.dtype), x[:, :-1, :]], axis=1)
            xr = mu_r * x + (1.0 - mu_r) * x_prev
            xk = mu_k * x + (1.0 - mu_k) * x_prev
            r = jax.nn.sigmoid(jnp.einsum('btc,dc->btd', xr, W_r))
            k = jnp.einsum('btc,dc->btd', xk, W_k)
            k_act = jnp.square(jax.nn.relu(k))
            out = r * jnp.einsum('btc,dc->btd', k_act, W_v)
            new_state = x[:, -1, :]
            return (out, new_state)
        key = jax.random.key(seed)
        ks = jax.random.split(key, 6)
        B, T, C = (8, 1024, DIM)
        x = jax.random.normal(ks[0], (B, T, C), dtype=jnp.float32)
        s = 1.0 / np.sqrt(C)
        W_r = jax.random.uniform(ks[1], (C, C), jnp.float32, -s, s)
        W_k = jax.random.uniform(ks[2], (C, C), jnp.float32, -s, s)
        W_v = jax.random.uniform(ks[3], (C, C), jnp.float32, -s, s)
        mu_r = jax.random.uniform(ks[4], (C,), jnp.float32)
        mu_k = jax.random.uniform(ks[5], (C,), jnp.float32)
        return {'x': x, 'W_r': W_r, 'W_k': W_k, 'W_v': W_v, 'mu_r': mu_r, 'mu_k': mu_k}
    _L0_ffn_in = _L0_ffn_setup()
    _d = {'L0_attn_x': _L0_attn_in['x'], 'L0_attn_Wk': _L0_attn_in['Wk'], 'L0_attn_bk': _L0_attn_in['bk'], 'L0_attn_Wv': _L0_attn_in['Wv'], 'L0_attn_bv': _L0_attn_in['bv'], 'L0_attn_Wq': _L0_attn_in['Wq'], 'L0_attn_bq': _L0_attn_in['bq'], 'L0_attn_gamma': _L0_attn_in['gamma'], 'L0_attn_beta': _L0_attn_in['beta'], 'L0_ffn_W_r': _L0_ffn_in['W_r'], 'L0_ffn_W_k': _L0_ffn_in['W_k'], 'L0_ffn_W_v': _L0_ffn_in['W_v'], 'L0_ffn_mu_r': _L0_ffn_in['mu_r'], 'L0_ffn_mu_k': _L0_ffn_in['mu_k']}
    _x0 = _d['L0_attn_x']
    _d['L0_attn_x'] = jax.random.normal(jax.random.fold_in(jax.random.key(seed), 1), (2, 4096, 512), dtype=_x0.dtype)
    del _x0
    return _d

def reference(L0_attn_x, L0_attn_Wk, L0_attn_bk, L0_attn_Wv, L0_attn_bv, L0_attn_Wq, L0_attn_bq, L0_attn_gamma, L0_attn_beta, L0_ffn_W_r, L0_ffn_W_k, L0_ffn_W_v, L0_ffn_mu_r, L0_ffn_mu_k):

    def _L0_attn_ref(x, Wk, bk, Wv, bv, Wq, bq, gamma, beta):
        import jax, jax.numpy as jnp
        import numpy as np
        TTT_LR = 0.01
        LN_EPS = 1e-05
        B, S, D = x.shape
        DS = Wk.shape[0]
        mu = jnp.mean(x, axis=-1, keepdims=True)
        var = jnp.mean((x - mu) ** 2, axis=-1, keepdims=True)
        h = (x - mu) * jax.lax.rsqrt(var + LN_EPS) * gamma + beta
        keys = jnp.einsum('bsd,ed->bse', h, Wk) + bk
        values = jnp.einsum('bsd,ed->bse', h, Wv) + bv
        queries = jnp.einsum('bsd,ed->bse', h, Wq) + bq

        def step(W, qkv):
            q_t, k_t, v_t = qkv
            y_t = jnp.einsum('bds,bs->bd', W, q_t)
            pred = jnp.einsum('bds,bs->bd', W, k_t)
            err = pred - v_t
            W = W - TTT_LR * err[:, :, None] * k_t[:, None, :]
            return (W, y_t)
        W0 = jnp.zeros((B, D, DS), x.dtype)
        qs = jnp.swapaxes(queries, 0, 1)
        ks_ = jnp.swapaxes(keys, 0, 1)
        vs = jnp.swapaxes(values, 0, 1)
        _, ys = jax.lax.scan(step, W0, (qs, ks_, vs))
        y = jnp.swapaxes(ys, 0, 1)
        return x + y

    def _L0_ffn_ref(x, W_r, W_k, W_v, mu_r, mu_k):
        import jax, jax.numpy as jnp
        import numpy as np
        DIM = 512

        def _reference_tuple_inner(x, W_r, W_k, W_v, mu_r, mu_k):
            B, T, C = x.shape
            x_prev = jnp.concatenate([jnp.zeros((B, 1, C), x.dtype), x[:, :-1, :]], axis=1)
            xr = mu_r * x + (1.0 - mu_r) * x_prev
            xk = mu_k * x + (1.0 - mu_k) * x_prev
            r = jax.nn.sigmoid(jnp.einsum('btc,dc->btd', xr, W_r))
            k = jnp.einsum('btc,dc->btd', xk, W_k)
            k_act = jnp.square(jax.nn.relu(k))
            out = r * jnp.einsum('btc,dc->btd', k_act, W_v)
            new_state = x[:, -1, :]
            return (out, new_state)
        return _reference_tuple_inner(x, W_r, W_k, W_v, mu_r, mu_k)[0]
    x = L0_attn_x
    xn = _layernorm(x, axis=-1)
    s = _L0_attn_ref(xn, L0_attn_Wk, L0_attn_bk, L0_attn_Wv, L0_attn_bv, L0_attn_Wq, L0_attn_bq, L0_attn_gamma, L0_attn_beta)
    g = _silu(_L0_ffn_ref(xn, L0_ffn_W_r, L0_ffn_W_k, L0_ffn_W_v, L0_ffn_mu_r, L0_ffn_mu_k))
    x = x + s * g
    return x

_drawn_inputs = setup_inputs


def setup_inputs(seed=0):
    import zlib

    import numpy as np

    out = dict(_drawn_inputs(seed))
    spreads = {'L0_attn_bk': (0.0, 0.1),
     'L0_attn_bv': (0.0, 0.8),
     'L0_attn_bq': (0.0, 0.465),
     'L0_attn_gamma': (1.0, 0.2),
     'L0_attn_beta': (0.0, 0.1)}
    factors = {'L0_ffn_mu_r': 2.817}
    for name, (base, spread) in spreads.items():
        noise = np.random.default_rng([zlib.crc32(name.encode()), seed]).standard_normal(out[name].shape)
        drawn = base * np.exp(spread * noise) if base else spread * noise
        out[name] = jnp.asarray(drawn.astype(out[name].dtype))
    for name, factor in factors.items():
        out[name] = (out[name] * factor).astype(out[name].dtype)
    return out
```

```python
from contextlib import ExitStack

import concourse.bass as bass
from concourse import mybir

F32 = mybir.dt.float32
F32R = mybir.dt.float32r
ALU = mybir.AluOpType
ACT = mybir.ActivationFunctionType

LR = 0.01
EPS = 1e-5


class Tile:

    def __init__(self, pair, off):
        self.pair, self.off = pair, off
        self.par = off % 2

    def __add__(self, n):
        return Tile(self.pair, self.off + n)

    def nth(self, per, k):
        n = per * self.off + k
        return n if isinstance(self.pair, int) else self.pair * (2 * per) + n

    def pos(self):
        return self.off // 2 if isinstance(self.pair, int) else self.pair + self.off // 2


def build(nc, x, Wk_t, bk, Wv_t, bv, Wq_t, bq, gamma, beta, Wr_t, Wfk_t, Wfv_t, mu_r, mu_k, out):
    P = 128
    B, S, D = x.shape
    DS = Wk_t.shape[1]
    KQ = 2 * DS
    CC = D // P
    C = P
    J = 2
    TT = J * C
    assert B == 2 and KQ == P
    NT = B * S // TT
    LEVELS = 6
    assert 2 ** (LEVELS + 1) == C

    x_v = x.rearrange("b (n q) d -> b n q d", q=TT)
    out_v = out.rearrange("b (n q) d -> b n q d", q=C)

    def w_view(w):
        return w.rearrange("(c p) n -> p c n", p=P)

    ctx = ExitStack()
    with ctx:
        def sb(name, shape, dt=F32):
            return ctx.enter_context(nc.sbuf_tensor(name, shape, dt))[:]

        def pb(name):
            return ctx.enter_context(nc.psum_tensor(name, [P, 512], F32))[:]

        def sem(name):
            return ctx.enter_context(nc.semaphore(name))

        def halves(name, shape):
            return sb(name + "_hi", shape, F32R), sb(name + "_lo", shape, F32R)

        wkq = halves("wkq", [P, CC, KQ])
        wv = halves("wv", [P, CC, D])
        wr = halves("wr", [P, CC, D])
        wfk = halves("wfk", [P, CC, D])
        wfv = halves("wfv", [P, CC, D])
        cols = sb("cols", [P, 4, CC])
        bias_v = sb("bias_v", [P, D])
        bias_kq = sb("bias_kq", [P, KQ])
        ident = sb("ident", [P, P])
        upper = sb("upper", [P, P])
        upper_lr = sb("upper_lr", [P, P])
        lower_lr = sb("lower_lr", [P, P])
        spare = sb("spare", [P, 1])
        small = sb("small", [P, 4, J])
        ones = sb("ones", [P, 4, J])

        x_in = sb("x_in", [P, J, D])
        bn = sb("bn", [P, J, 6])
        mv = sb("mv", [P, J, 2])
        st = sb("st", [P, 4, J])
        st_tmp = sb("st_tmp", [P, 4, J])
        st_keep = [sb(f"st_keep{i}", [P, 4, J]) for i in range(2)]
        xn = sb("xn", [P, J, D])
        xt = sb("xt", [P, CC, TT + 1])
        carry = [sb(f"carry{i}", [P, CC, 1]) for i in range(2)]
        dx = sb("dx", [P, CC, TT])
        mix = sb("mix", [P, CC // 2, TT])
        xnT = halves("xnT", [P, CC, TT])
        xkT = halves("xkT", [P, CC, TT])
        xrT = halves("xrT", [P, CC, TT])

        kq32 = sb("kq32", [P, J, KQ])
        kn = [sb(f"kn{i}", [P, J, 5 * DS], F32R) for i in range(2)]
        qn = sb("qn", [P, J, 2 * DS], F32R)
        kqT = [sb(f"kqT{i}", [P, J, 3, C], F32R) for i in range(2)]
        v32 = sb("v32", [P, J, D])
        v = [halves(f"v{i}", [P, J, D]) for i in range(2)]
        at32 = kq32
        beta_b = v32[:, 0].rearrange("p (c q) -> p c q", c=CC)
        at = [halves(f"at{i}", [P, J, C]) for i in range(2)]
        px = sb("px", [P, J, 2, C])
        pt = sb("pt", [P, J, C])
        tT = halves("tT", [P, J, C])
        kp = sb("kp", [P, J, C], F32R)
        act32 = sb("act32", [P, CC, TT])
        actT = halves("actT", [P, CC, TT])
        gate_r = sb("gate_r", [P, J, D])
        g = sb("g", [P, 2, J, D])

        s_hi = [sb(f"s_hi{i}", [P, D], F32R) for i in range(2)]
        s_lo = [sb(f"s_lo{i}", [P, D], F32R) for i in range(2)]
        u = halves("u", [P, D])
        x_res = sb("x_res", [P, 2, J, D])
        o = sb("o", [P, J, D])

        s_ps = [pb(f"s_ps{i}") for i in range(2)]
        u_ps = pb("u_ps")
        y_ps = pb("y_ps")
        f_ps = [pb(f"f_ps{i}") for i in range(2)]
        a_ps = pb("a_ps")
        b_ps = pb("b_ps")

        cols_ld = sem("cols_ld")
        bias_ld = sem("bias_ld")
        w_ld = [sem(f"w_ld{i}") for i in range(2)]
        x_ld = sem("x_ld")
        xres_ld = [sem(f"xres_ld{i}") for i in range(2)]
        out_st = [sem(f"out_st{i}") for i in range(J)]
        const0 = sem("const0")
        consts = sem("consts")
        dve_zero = sem("dve_zero")
        s_zero = sem("s_zero")
        beta_bc = sem("beta_bc")
        bias_mm = sem("bias_mm")
        bias_add = sem("bias_add")
        bias_done = sem("bias_done")
        w_fold = sem("w_fold")
        w_hi = sem("w_hi")
        w_lo = sem("w_lo")
        bn_done = sem("bn_done")
        mv_done = sem("mv_done")
        st_step = sem("st_step")
        st_done = sem("st_done")
        kept = sem("kept")
        xn_done = sem("xn_done")
        xt_mm = sem("xt_mm")
        carried = sem("carried")
        xt_first = sem("xt_first")
        xt_ev = sem("xt_ev")
        xnT_hi = sem("xnT_hi")
        xnT_lo = sem("xnT_lo")
        dx_done = sem("dx_done")
        xk_mix = sem("xk_mix")
        xk_hi = sem("xk_hi")
        xk_lo = sem("xk_lo")
        xr_mix = sem("xr_mix")
        xr_hi = sem("xr_hi")
        xr_lo = sem("xr_lo")
        kq_mm = sem("kq_mm")
        kq_ev = sem("kq_ev")
        kn_hi = sem("kn_hi")
        kn_lo = sem("kn_lo")
        qn_hi = sem("qn_hi")
        qn_lo = sem("qn_lo")
        kqT_mm = sem("kqT_mm")
        kqT_ev = sem("kqT_ev")
        g_mm = sem("g_mm")
        m_ev = sem("m_ev")
        mt_ev = sem("mt_ev")
        x0_done = sem("x0_done")
        at_ev = sem("at_ev")
        at_hi = sem("at_hi")
        at_lo = sem("at_lo")
        lv_mm = sem("lv_mm")
        lt_mm = sem("lt_mm")
        p_ev = sem("p_ev")
        pt_ev = sem("pt_ev")
        x_up = sem("x_up")
        t_hi = sem("t_hi")
        t_lo = sem("t_lo")
        kp_mm = sem("kp_mm")
        kp_hi = sem("kp_hi")
        kp_lo = sem("kp_lo")
        v_mm = sem("v_mm")
        v_ev = sem("v_ev")
        v_hi = sem("v_hi")
        v_lo = sem("v_lo")
        k_mm = sem("k_mm")
        relu_ev = sem("relu_ev")
        square = sem("square")
        act_hi = sem("act_hi")
        act_lo = sem("act_lo")
        r_mm = sem("r_mm")
        r_ev = sem("r_ev")
        kv_mm = sem("kv_mm")
        mix_ev = sem("mix_ev")
        sig = sem("sig")
        g_done = sem("g_done")
        u_mm = sem("u_mm")
        u_hi = sem("u_hi")
        u_lo = sem("u_lo")
        s_mm = sem("s_mm")
        sc_hi = sem("sc_hi")
        sc_lo = sem("sc_lo")
        y_mm = sem("y_mm")
        xn_again = sem("xn_again")
        y_add = sem("y_add")
        gated = sem("gated")
        o_done = sem("o_done")

        stage = [x_res[:, :, :, :].rearrange("p a j d -> p (a j) d"),
                 g[:, :, :, :].rearrange("p a j d -> p (a j) d")]
        WEIGHTS = [(wkq, KQ), (wv, D), (wfk, D), (wr, D), (wfv, D)]
        NW = len(WEIGHTS)

        def staged(n):
            return stage[n % 2][:, :, 0:WEIGHTS[n][1]]

        def w_count(n):
            return 16 * (n // 2 + 1) + (16 if n % 2 == 0 else 0)

        PAIRS = (NT - 2) // 2

        block = ctx.enter_context(nc.Block())

        @block.sync
        def _(sp):
            def load_x(n):
                if not (isinstance(n.pair, int) and n.off < 1):
                    sp.wait_ge(xn_done, n.nth(1, 0))
                sp.dma_start(x_in, x_v[n.par, bass.ds(n.pos(), 1), :, :].rearrange(
                    "a (j q) d -> q (a j) d", q=C)).then_inc(x_ld, 16)

            def load_x_res(t):
                if isinstance(t.pair, int) and t.off < 2:
                    sp.wait_ge(w_lo, NW)
                else:
                    sp.wait_ge(o_done, (t + -1).nth(J, 0))
                sp.dma_start(x_res[:, t.par], x_v[t.par, bass.ds(t.pos(), 1), :, :].rearrange(
                    "a (j q) d -> q (a j) d", q=C)).then_inc(xres_ld[t.par], 16)

            def store(p, j):
                sp.wait_ge(o_done, p.nth(J, j + 1))
                sp.dma_start(out_v[p.par, bass.ds(p.pos() * J + j, 1), :, :].rearrange("a q d -> q (a d)"),
                             o[:, j]).then_inc(out_st[j], 16)

            def step(t, main=True, prev=True, ahead=True):
                if ahead:
                    load_x(t + 1)
                if main:
                    load_x_res(t)
                if prev:
                    for j in range(J):
                        store(t + -1, j)

            load_x(Tile(0, 0))
            for n, w in enumerate(((Wk_t, Wq_t), Wv_t, Wfk_t, Wr_t, Wfv_t)):
                if n >= 2:
                    sp.wait_ge(w_lo, n - 1)
                if n == 0:
                    for i, part in enumerate(w):
                        sp.dma_start(staged(0)[:, :, i * DS:(i + 1) * DS], w_view(part)).then_inc(w_ld[0], 16)
                else:
                    sp.dma_start(staged(n), w_view(w)).then_inc(w_ld[n % 2], 16)
            step(Tile(0, 0), prev=False)
            with sp.Fori(0, PAIRS) as i:
                for b in range(2):
                    step(Tile(i, 1 + b))
            step(Tile(0, NT - 1), ahead=False)
            step(Tile(0, NT), main=False, ahead=False)
            for j in range(J):
                sp.wait_ge(out_st[j], 16 * NT)

        @block.gpsimd
        def _(pool):
            nc.gpsimd.memset(ident, 0.0)
            nc.gpsimd.memset(upper, 1.0)
            nc.gpsimd.memset(upper_lr, -LR)
            nc.gpsimd.memset(lower_lr, -LR)
            for k, value in enumerate((EPS, LR, -0.5, 1.0)):
                nc.gpsimd.memset(small[:, k], value)
            nc.gpsimd.memset(ones, 1.0).then_inc(const0, 1)
            pool.wait_ge(const0, 1)
            nc.gpsimd.affine_select(out=ident, in_=ident, compare_op=ALU.not_equal, fill=1.0, base=0,
                                    pattern=[[-1, P]], channel_multiplier=1)
            for m in (upper, upper_lr):
                nc.gpsimd.affine_select(out=m, in_=m, compare_op=ALU.is_gt, fill=0.0, base=0,
                                        pattern=[[1, P]], channel_multiplier=-1)
            nc.gpsimd.affine_select(out=lower_lr, in_=lower_lr, compare_op=ALU.is_gt, fill=0.0, base=0,
                                    pattern=[[-1, P]], channel_multiplier=1).then_inc(consts, 1)
            pool.wait_ge(consts, 1)

            def norm_scalars(n):
                steps = 7
                mean, var = mv[:, :, 0], mv[:, :, 1]
                eps, lr, power, one = (small[:, k] for k in range(4))
                pool.wait_ge(mv_done, n.nth(1, 1))
                if not (isinstance(n.pair, int) and n.off < 1):
                    pool.wait_ge(kept, n.nth(1, 0))
                    pool.wait_ge(xn_done, n.nth(1, 0))
                nc.gpsimd.tensor_tensor(st[:, 0], mean, one, ALU.mult).then_inc(st_step, 1)
                nc.gpsimd.tensor_tensor(st_tmp[:, 0], var, eps, ALU.add).then_inc(st_step, 1)
                pool.wait_ge(st_step, n.nth(steps, 2))
                nc.gpsimd.tensor_tensor(st[:, 1], st_tmp[:, 0], power, ALU.pow).then_inc(st_step, 1)
                pool.wait_ge(st_step, n.nth(steps, 3))
                nc.gpsimd.tensor_tensor(st_tmp[:, 1], st[:, 1], st[:, 1], ALU.mult).then_inc(st_step, 1)
                pool.wait_ge(st_step, n.nth(steps, 4))
                nc.gpsimd.tensor_tensor(st_tmp[:, 2], st_tmp[:, 1], var, ALU.mult).then_inc(st_step, 1)
                pool.wait_ge(st_step, n.nth(steps, 5))
                nc.gpsimd.tensor_tensor(st_tmp[:, 3], st_tmp[:, 2], eps, ALU.add).then_inc(st_step, 1)
                pool.wait_ge(st_step, n.nth(steps, 6))
                nc.gpsimd.tensor_tensor(st[:, 2], st_tmp[:, 3], power, ALU.pow).then_inc(st_step, 1)
                pool.wait_ge(st_step, n.nth(steps, 7))
                nc.gpsimd.tensor_tensor(st[:, 3], st[:, 2], lr, ALU.mult).then_inc(st_done, 1)

            def shift_difference(n):
                pool.wait_ge(xt_ev, n.nth(J, 2))
                pool.wait_ge(xt_first, n.nth(1, 1))
                if not (isinstance(n.pair, int) and n.off < 1):
                    pool.wait_ge(xr_mix, n.nth(2, 0))
                nc.gpsimd.tensor_tensor(dx, xt[:, :, 1:TT + 1], xt[:, :, 0:TT], ALU.subtract).then_inc(dx_done, 1)

            def keep_scalars(t):
                if not (isinstance(t.pair, int) and t.off < 2):
                    pool.wait_ge(xn_again, (t + -1).nth(J, 0))
                pool.wait_ge(st_done, t.nth(1, 1))
                nc.gpsimd.tensor_tensor(st_keep[t.par], st, ones, ALU.mult).then_inc(kept, 1)

            def v_low(t, j):
                pool.wait_ge(v_hi, t.nth(J, j + 1))
                nc.gpsimd.tensor_tensor(v[t.par][1][:, j], v32[:, j], v[t.par][0][:, j].bitcast(F32),
                                        ALU.subtract).then_inc(v_lo, 1)

            def at_low(t):
                pool.wait_ge(at_hi, t.nth(1, 1))
                nc.gpsimd.tensor_tensor(at[t.par][1], at32, at[t.par][0].bitcast(F32),
                                        ALU.subtract).then_inc(at_lo, 1)

            def act_low(t, m):
                half = slice(m * CC // 2, (m + 1) * CC // 2)
                pool.wait_ge(act_hi, t.nth(2, m + 1))
                if not (isinstance(t.pair, int) and t.off < 1):
                    pool.wait_ge(kv_mm, t.nth(J, 0))
                nc.gpsimd.tensor_tensor(actT[1][:, half], act32[:, half], actT[0][:, half].bitcast(F32),
                                        ALU.subtract).then_inc(act_lo, 1)

            def silu(t, j):
                pool.wait_ge(sig, t.nth(J, j + 1))
                nc.gpsimd.tensor_tensor(g[:, t.par, j], g[:, t.par, j], gate_r[:, j], ALU.mult).then_inc(g_done, 1)

            def output(p, j):
                pool.wait_ge(y_add, p.nth(J, j + 1))
                pool.wait_ge(g_done, p.nth(J, j + 1))
                nc.gpsimd.tensor_tensor(o[:, j], o[:, j], g[:, p.par, j], ALU.mult).then_inc(gated, 1)
                pool.wait_ge(gated, p.nth(J, j + 1))
                nc.gpsimd.tensor_tensor(o[:, j], o[:, j], x_res[:, p.par, j], ALU.add).then_inc(o_done, 1)

            def step(t, main=True, prev=True, nxt=True):
                p, n = t + -1, t + 1
                if main:
                    keep_scalars(t)
                if nxt:
                    norm_scalars(n)
                if main:
                    v_low(t, 0)
                if prev:
                    output(p, 0)
                if main:
                    v_low(t, 1)
                    at_low(t)
                    act_low(t, 0)
                if nxt:
                    shift_difference(n)
                if main:
                    act_low(t, 1)
                if prev:
                    output(p, 1)
                if main:
                    silu(t, 0)
                    silu(t, 1)

            norm_scalars(Tile(0, 0))
            shift_difference(Tile(0, 0))
            step(Tile(0, 0), prev=False)
            with pool.Fori(0, PAIRS) as i:
                for b in range(2):
                    step(Tile(i, 1 + b))
            step(Tile(0, NT - 1), nxt=False)
            step(Tile(0, NT), main=False, nxt=False)

        @block.scalar
        def _(act):
            act.dma_start(cols[:, 0], gamma).then_inc(cols_ld, 16)
            act.dma_start(cols[:, 1], beta).then_inc(cols_ld, 16)
            act.dma_start(cols[:, 2], mu_r).then_inc(cols_ld, 16)
            act.dma_start(cols[:, 3], mu_k).then_inc(cols_ld, 16)
            act.dma_start(bias_v, bv.partition_broadcast(P)).then_inc(bias_ld, 16)
            act.dma_start(bias_kq[:, 0:DS], bk.partition_broadcast(P)).then_inc(bias_ld, 16)
            act.dma_start(bias_kq[:, DS:KQ], bq.partition_broadcast(P)).then_inc(bias_ld, 16)

            def copy(out_, in_, **kw):
                return nc.scalar.activation(out_, in_, ACT.Copy, **kw)

            for n in range(NW):
                if n < 2:
                    act.wait_ge(w_fold, n + 1)
                else:
                    act.wait_ge(w_ld[n % 2], w_count(n))
                copy(WEIGHTS[n][0][0], staged(n)).then_inc(w_hi, 1)

            def transposed(n, j):
                act.wait_ge(xt_mm, n.nth(J, j + 1))
                if j == 0 and not (isinstance(n.pair, int) and n.off < 1):
                    act.wait_ge(carried, n.nth(1, 0))
                    act.wait_ge(xr_mix, n.nth(2, 0))
                    act.wait_ge(xnT_lo, n.nth(1, 0))
                f = f_ps[(11 * (n.off - 1) + (3 if j == 0 else 5)) % 2] if n.off else f_ps[j]
                copy(xt[:, :, 1 + j * C:1 + (j + 1) * C],
                     f.rearrange("p (c q) -> p c q", c=CC)).then_inc(xt_ev, 1)

            def kqT_copy(t, j):
                act.wait_ge(kqT_mm, t.nth(J, j + 1))
                src = (b_ps, a_ps)[j]
                copy(kqT[t.par][:, j], src[:, 0:3 * C].rearrange("p (k q) -> p k q", k=3)).then_inc(kqT_ev, 1)

            def v_high(t, j):
                act.wait_ge(v_ev, t.nth(J, j + 1))
                copy(v[t.par][0][:, j], v32[:, j]).then_inc(v_hi, 1)

            def at_high(t):
                act.wait_ge(at_ev, t.nth(1, 1))
                copy(at[t.par][0], at32).then_inc(at_hi, 1)

            def power(t, i):
                if i == 1:
                    act.wait_ge(x0_done, t.nth(1, 1))
                act.wait_ge(lv_mm, t.nth(LEVELS + 1, i))
                src = a_ps.rearrange("p (j k q) -> p j k q", j=J, k=2)
                copy(px[:, :, 0], src[:, :, 0]).then_inc(p_ev, 1)

            def power_transposed(t, i):
                act.wait_ge(lt_mm, t.nth(LEVELS, i))
                copy(pt, b_ps[:, 0:J * C].rearrange("p (j q) -> p j q", j=J)).then_inc(pt_ev, 1)

            def t_high(p):
                act.wait_ge(x_up, p.nth(LEVELS, LEVELS))
                if not (isinstance(p.pair, int) and p.off < 1):
                    act.wait_ge(u_mm, p.nth(J, 0))
                copy(tT[0], px[:, :, 1]).then_inc(t_hi, 1)

            def kp_high(p):
                act.wait_ge(kp_mm, p.nth(1, 1))
                copy(kp, b_ps[:, 0:J * C].rearrange("p (j q) -> p j q", j=J), scale=-LR).then_inc(kp_hi, 1)

            def u_high(p, j):
                act.wait_ge(u_mm, p.nth(J, j + 1))
                if j or not (isinstance(p.pair, int) and p.off < 1):
                    act.wait_ge(y_mm, p.nth(J, j))
                copy(u[0], u_ps).then_inc(u_hi, 1)

            def s_high(p, j):
                act.wait_ge(s_mm, p.nth(J, j + 1))
                copy(s_hi[p.par], s_ps[p.par]).then_inc(sc_hi, 1)

            def relu(t, m):
                act.wait_ge(k_mm, t.nth(2, m + 1))
                if not (isinstance(t.pair, int) and t.off < 1):
                    act.wait_ge(act_lo, t.nth(2, 0))
                nc.scalar.activation(act32[:, 2 * m:2 * m + 2], f_ps[(11 * t.off + (4 if m == 0 else 6)) % 2]
                                     .rearrange("p (c q) -> p c q", c=2), ACT.Relu).then_inc(relu_ev, 1)

            def act_high(t, m):
                act.wait_ge(square, t.nth(2, m + 1))
                if not (isinstance(t.pair, int) and t.off < 1):
                    act.wait_ge(kv_mm, t.nth(J, 0))
                copy(actT[0][:, 2 * m:2 * m + 2], act32[:, 2 * m:2 * m + 2]).then_inc(act_hi, 1)

            def sigmoid_r(t, j):
                act.wait_ge(r_mm, t.nth(J, j + 1))
                if not (isinstance(t.pair, int) and t.off < 1):
                    act.wait_ge(g_done, t.nth(J, 0))
                nc.scalar.activation(gate_r[:, j], f_ps[(11 * t.off + 7 + j) % 2], ACT.Sigmoid).then_inc(r_ev, 1)

            def sigmoid_mix(t, j):
                act.wait_ge(mix_ev, t.nth(J, j + 1))
                nc.scalar.activation(gate_r[:, j], g[:, t.par, j], ACT.Sigmoid).then_inc(sig, 1)

            def step(t, main=True, prev=True, nxt=True):
                p, n = t + -1, t + 1
                if prev:
                    t_high(p)
                    kp_high(p)
                if main:
                    v_high(t, 0)
                    kqT_copy(t, 0)
                if prev:
                    u_high(p, 0)
                if main:
                    kqT_copy(t, 1)
                if prev:
                    s_high(p, 0)
                if main:
                    at_high(t)
                    v_high(t, 1)
                    power(t, 1)
                if nxt:
                    transposed(n, 0)
                if main:
                    power_transposed(t, 1)
                    relu(t, 0)
                    power(t, 2)
                if prev:
                    u_high(p, 1)
                if main:
                    act_high(t, 0)
                if nxt:
                    transposed(n, 1)
                if main:
                    power_transposed(t, 2)
                    power(t, 3)
                if prev:
                    s_high(p, 1)
                if main:
                    relu(t, 1)
                    power_transposed(t, 3)
                    act_high(t, 1)
                    power(t, 4)
                    sigmoid_r(t, 0)
                    power_transposed(t, 4)
                    power(t, 5)
                    sigmoid_r(t, 1)
                    power_transposed(t, 5)
                    power(t, 6)
                    sigmoid_mix(t, 0)
                    power_transposed(t, 6)
                    sigmoid_mix(t, 1)

            for j in range(J):
                transposed(Tile(0, 0), j)
            step(Tile(0, 0), prev=False)
            with act.Fori(0, PAIRS) as i:
                for b in range(2):
                    step(Tile(i, 1 + b))
            step(Tile(0, NT - 1), nxt=False)
            step(Tile(0, NT), main=False, nxt=False)

        @block.vector
        def _(dve):
            V = nc.vector

            def rounded(out_, in_):
                return V.tensor_copy(out_, in_)

            def rest(out_, in_, hi):
                return V.tensor_tensor(out_, in_, hi.bitcast(F32), ALU.subtract)

            for i in range(2):
                V.memset(s_hi[i].bitcast(F32), 0.0)
                V.memset(s_lo[i].bitcast(F32), 0.0)
                V.memset(carry[i], 0.0)
            V.memset(xt[:, :, 0:1], 0.0).then_inc(dve_zero, 1)
            dve.wait_ge(cols_ld, 64)
            V.tensor_copy(beta_b, cols[:, 1].unsqueeze(2).to_broadcast([P, CC, P])).then_inc(beta_bc, 1)
            dve.wait_ge(bias_ld, 48)
            for n, bias in ((0, bias_kq), (1, bias_v)):
                wide = WEIGHTS[n][1]
                dve.wait_ge(bias_mm, n + 1)
                V.tensor_tensor(bias, f_ps[n][:, 0:wide], bias, ALU.add).then_inc(bias_add, 1)
                for c in range(CC):
                    last = V.tensor_scalar(staged(n)[:, c], staged(n)[:, c], cols[:, 0, c:c + 1], None, ALU.mult)
                last.then_inc(w_fold, 1)
            dve.wait_ge(bias_add, 2)
            V.tensor_scalar(bias_v, bias_v, LR, None, ALU.mult).then_inc(bias_done, 1)
            for n in range(NW):
                dve.wait_ge(w_hi, n + 1)
                rest(WEIGHTS[n][0][1], staged(n), WEIGHTS[n][0][0]).then_inc(w_lo, 1)

            def stats(n):
                dve.wait_ge(x_ld, n.nth(16, 16))
                for j in range(J):
                    last = V.bn_stats(bn[:, j], x_in[:, j])
                last.then_inc(bn_done, 1)
                if not (isinstance(n.pair, int) and n.off < 1):
                    dve.wait_ge(st_done, n.nth(1, 0))
                dve.wait_ge(bn_done, n.nth(1, 1))
                V.memset(spare, 0.0)
                for j in range(J):
                    last = V.bn_aggr(mv[:, j], bn[:, j])
                last.then_inc(mv_done, 1)

            def normalise(n):
                dve.wait_ge(st_done, n.nth(1, 1))
                if not (isinstance(n.pair, int) and n.off < 1):
                    dve.wait_ge(xt_mm, n.nth(J, 0))
                for j in range(J):
                    last = V.tensor_scalar(xn[:, j], x_in[:, j], st[:, 0, j:j + 1], st[:, 1, j:j + 1],
                                           ALU.subtract, ALU.mult)
                last.then_inc(xn_done, 1)

            def carry_over(n):
                before = n + -1
                dve.wait_ge(xt_ev, before.nth(J, 2))
                V.tensor_copy(carry[before.par], xt[:, :, TT:TT + 1]).then_inc(carried, 1)

            def first_column(n):
                if not (isinstance(n.pair, int) and n.off < 1):
                    dve.wait_ge(carried, n.nth(1, 0))
                    dve.wait_ge(dx_done, n.nth(1, 0))
                    dve.wait_ge(xr_mix, n.nth(2, 0))
                V.tensor_copy(xt[:, :, 0:1], carry[n.par]).then_inc(xt_first, 1)

            def xn_halves(n):
                dve.wait_ge(xt_ev, n.nth(J, 2))
                if not (isinstance(n.pair, int) and n.off < 1):
                    dve.wait_ge(v_mm, n.nth(J, 0))
                rounded(xnT[0], xt[:, :, 1:TT + 1]).then_inc(xnT_hi, 1)
                dve.wait_ge(xnT_hi, n.nth(1, 1))
                rest(xnT[1], xt[:, :, 1:TT + 1], xnT[0]).then_inc(xnT_lo, 1)

            def mixed(n, m, dst, mu, made, hi, lo):
                for i in range(CC // 2):
                    c = m * (CC // 2) + i
                    last = V.scalar_tensor_tensor(mix[:, i], dx[:, c], cols[:, mu, c:c + 1], xt[:, c, 0:TT],
                                                  ALU.mult, ALU.add)
                last.then_inc(made, 1)
                part = slice(m * (CC // 2), (m + 1) * (CC // 2))
                dve.wait_ge(made, n.nth(2, m + 1))
                rounded(dst[0][:, part], mix).then_inc(hi, 1)
                dve.wait_ge(hi, n.nth(2, m + 1))
                rest(dst[1][:, part], mix, dst[0][:, part]).then_inc(lo, 1)

            def key_mix(n, m):
                if m:
                    dve.wait_ge(xk_lo, n.nth(2, 1))
                else:
                    dve.wait_ge(dx_done, n.nth(1, 1))
                    dve.wait_ge(xt_first, n.nth(1, 1))
                    if not (isinstance(n.pair, int) and n.off < 1):
                        dve.wait_ge(k_mm, n.nth(2, 0))
                mixed(n, m, xkT, 3, xk_mix, xk_hi, xk_lo)

            def gate_mix(n, m):
                if m:
                    dve.wait_ge(xr_lo, n.nth(2, 1))
                else:
                    dve.wait_ge(xk_lo, n.nth(2, 2))
                    if not (isinstance(n.pair, int) and n.off < 1):
                        dve.wait_ge(r_mm, n.nth(J, 0))
                mixed(n, m, xrT, 2, xr_mix, xr_hi, xr_lo)

            def kq_rows(t):
                dve.wait_ge(kq_mm, t.nth(1, 1))
                dve.wait_ge(kept, t.nth(1, 1))
                if not (isinstance(t.pair, int) and t.off < 1):
                    dve.wait_ge(at_lo, t.nth(1, 0))
                f = f_ps[(11 * t.off) % 2]
                for j in range(J):
                    last = V.scalar_tensor_tensor(kq32[:, j], f[:, j * KQ:(j + 1) * KQ], st_keep[t.par][:, 2, j:j + 1],
                                                  bias_kq, ALU.mult, ALU.add)
                last.then_inc(kq_ev, 1)
                dve.wait_ge(kq_ev, t.nth(1, 1))
                rows = kn[t.par].rearrange("p j (b e) -> p j b e", e=DS)
                for j in range(J):
                    k32 = kq32[:, j, 0:DS].unsqueeze(1).to_broadcast([P, 2, DS])
                    last = rounded(rows[:, j, 0:2], k32)
                rounded(rows[:, :, 4], kq32[:, :, 0:DS]).then_inc(kn_hi, 1)
                rounded(qn[:, :, 0:DS], kq32[:, :, DS:KQ]).then_inc(qn_hi, 1)
                dve.wait_ge(kn_hi, t.nth(1, 1))
                for j in range(J):
                    k32 = kq32[:, j, 0:DS].unsqueeze(1).to_broadcast([P, 2, DS])
                    last = rest(rows[:, j, 2:4], k32, rows[:, j, 0:2])
                last.then_inc(kn_lo, 1)
                dve.wait_ge(qn_hi, t.nth(1, 1))
                rest(qn[:, :, DS:KQ], kq32[:, :, DS:KQ], qn[:, :, 0:DS]).then_inc(qn_lo, 1)

            def v_rows(t, j):
                dve.wait_ge(v_mm, t.nth(J, j + 1))
                if not (isinstance(t.pair, int) and t.off < 1):
                    dve.wait_ge(v_lo, t.nth(J, 0))
                V.scalar_tensor_tensor(v32[:, j], f_ps[(11 * t.off + 1 + j) % 2], st_keep[t.par][:, 3, j:j + 1],
                                       bias_v, ALU.mult, ALU.add).then_inc(v_ev, 1)

            def masked(t):
                dve.wait_ge(g_mm, t.nth(1, 1))
                src = a_ps.rearrange("p (j k q) -> p j k q", j=J, k=2)
                if not (isinstance(t.pair, int) and t.off < 1):
                    dve.wait_ge(t_lo, t.nth(1, 0))
                V.tensor_tensor(px[:, :, 0], src[:, :, 0], upper_lr.unsqueeze(1).to_broadcast([P, J, C]),
                                ALU.mult).then_inc(m_ev, 1)
                V.tensor_tensor(pt, src[:, :, 0], lower_lr.unsqueeze(1).to_broadcast([P, J, C]),
                                ALU.mult).then_inc(mt_ev, 1)
                V.tensor_tensor(at32, src[:, :, 1], upper.unsqueeze(1).to_broadcast([P, J, C]),
                                ALU.mult).then_inc(at_ev, 1)
                dve.wait_ge(m_ev, t.nth(1, 1))
                V.tensor_tensor(px[:, :, 1], px[:, :, 0], ident.unsqueeze(1).to_broadcast([P, J, C]),
                                ALU.add).then_inc(x0_done, 1)

            def factor(t, i):
                if i < LEVELS:
                    dve.wait_ge(p_ev, t.nth(LEVELS, i + 1))
                else:
                    dve.wait_ge(lv_mm, t.nth(LEVELS + 1, i + 1))
                if i == 1:
                    dve.wait_ge(x0_done, t.nth(1, 1))
                else:
                    dve.wait_ge(x_up, t.nth(LEVELS, i - 1))
                src = a_ps.rearrange("p (j k q) -> p j k q", j=J, k=2)
                V.tensor_tensor(px[:, :, 1], src[:, :, 1], px[:, :, 1], ALU.add).then_inc(x_up, 1)

            def t_low(p):
                dve.wait_ge(t_hi, p.nth(1, 1))
                rest(tT[1], px[:, :, 1], tT[0]).then_inc(t_lo, 1)

            def kp_low(p):
                dve.wait_ge(kp_hi, p.nth(1, 1))
                low = slice(DS, 2 * DS)
                V.scalar_tensor_tensor(kp[low], b_ps[low, 0:J * C].rearrange("p (j q) -> p j q", j=J), -LR,
                                       kp[low].bitcast(F32), ALU.mult, ALU.subtract).then_inc(kp_lo, 1)

            def u_low(p, j):
                dve.wait_ge(u_hi, p.nth(J, j + 1))
                rest(u[1], u_ps, u[0]).then_inc(u_lo, 1)

            def s_low(p, j):
                dve.wait_ge(sc_hi, p.nth(J, j + 1))
                rest(s_lo[p.par], s_ps[p.par], s_hi[p.par]).then_inc(sc_lo, 1)

            def squared(t, m):
                half = slice(m * CC // 2, (m + 1) * CC // 2)
                dve.wait_ge(relu_ev, t.nth(2, m + 1))
                V.tensor_tensor(act32[:, half], act32[:, half], act32[:, half], ALU.mult).then_inc(square, 1)

            def gated_mix(t, j):
                dve.wait_ge(kv_mm, t.nth(J, j + 1))
                dve.wait_ge(r_ev, t.nth(J, j + 1))
                if not (isinstance(t.pair, int) and t.off < 2):
                    dve.wait_ge(o_done, (t + -1).nth(J, 0))
                V.tensor_tensor(g[:, t.par, j], f_ps[(11 * t.off + 9 + j) % 2], gate_r[:, j],
                                ALU.mult).then_inc(mix_ev, 1)

            def xn_rebuilt(p, j):
                dve.wait_ge(xres_ld[p.par], (p.pos() + 1) * 16)
                if not (isinstance(p.pair, int) and p.off < 1):
                    dve.wait_ge(out_st[j], p.nth(16, 0))
                V.tensor_scalar(o[:, j], x_res[:, p.par, j], st_keep[p.par][:, 0, j:j + 1],
                                st_keep[p.par][:, 1, j:j + 1], ALU.subtract, ALU.mult).then_inc(xn_again, 1)

            def y_added(p, j):
                dve.wait_ge(y_mm, p.nth(J, j + 1))
                dve.wait_ge(xn_again, p.nth(J, j + 1))
                V.tensor_tensor(o[:, j], y_ps, o[:, j], ALU.add).then_inc(y_add, 1)

            def step(t, main=True, prev=True, nxt=True):
                p, n = t + -1, t + 1
                if nxt:
                    stats(n)
                if prev:
                    factor(p, LEVELS)
                if main:
                    kq_rows(t)
                if prev:
                    t_low(p)
                    xn_rebuilt(p, 0)
                    kp_low(p)
                if main:
                    v_rows(t, 0)
                if prev:
                    u_low(p, 0)
                if nxt:
                    normalise(n)
                    carry_over(n)
                    first_column(n)
                if main:
                    masked(t)
                if prev:
                    s_low(p, 0)
                    y_added(p, 0)
                if main:
                    v_rows(t, 1)
                if prev:
                    xn_rebuilt(p, 1)
                if main:
                    factor(t, 1)
                    squared(t, 0)
                if prev:
                    u_low(p, 1)
                if nxt:
                    xn_halves(n)
                if main:
                    factor(t, 2)
                if prev:
                    s_low(p, 1)
                    y_added(p, 1)
                if main:
                    squared(t, 1)
                    factor(t, 3)
                if nxt:
                    key_mix(n, 0)
                    key_mix(n, 1)
                if main:
                    factor(t, 4)
                if nxt:
                    gate_mix(n, 0)
                if main:
                    factor(t, 5)
                    gated_mix(t, 0)
                if nxt:
                    gate_mix(n, 1)
                if main:
                    gated_mix(t, 1)

            first = Tile(0, 0)
            stats(first)
            normalise(first)
            first_column(first)
            xn_halves(first)
            for m in range(2):
                key_mix(first, m)
            for m in range(2):
                gate_mix(first, m)
            step(first, prev=False)
            with dve.Fori(0, PAIRS) as i:
                for b in range(2):
                    step(Tile(i, 1 + b))
            step(Tile(0, NT - 1), nxt=False)
            step(Tile(0, NT), main=False, nxt=False)

        @block.tensor
        def _(pe):
            def mm(out_, lhsT, rhs, start, stop):
                return nc.tensor.matmul(out_, lhsT, rhs, start=start, stop=stop)

            def split_mm(out_, w, m, start, stop):
                mm(out_, w[0], m[0], start, False)
                mm(out_, w[1], m[0], False, False)
                return mm(out_, w[0], m[1], False, stop)

            def cut(pair, *at_):
                return pair[0][at_], pair[1][at_]

            ALL = slice(None)

            pe.wait_ge(beta_bc, 1)
            for n in range(2):
                pe.wait_ge(w_ld[n], w_count(n))
                for c in range(CC):
                    last = mm(f_ps[n][:, 0:WEIGHTS[n][1]], beta_b[:, c], staged(n)[:, c], c == 0, c == CC - 1)
                last.then_inc(bias_mm, 1)
            pe.wait_ge(dve_zero, 1)
            for i in range(2):
                nc.tensor.matmul(s_ps[i], s_hi[i][:, 0:P], s_hi[i], start=True, stop=False,
                                 skip_group_check=True)

            def xn_transposes(n, j):
                pe.wait_ge(xn_done, n.nth(1, 1))
                if n.off == 0:
                    pe.wait_ge(bias_add, 2)
                    f = f_ps[j]
                elif j == 0:
                    pe.wait_ge(v_ev, (n + -1).nth(J, 1))
                    f = f_ps[(11 * (n.off - 1) + 3) % 2]
                else:
                    pe.wait_ge(xt_ev, n.nth(J, 1))
                    f = f_ps[(11 * (n.off - 1) + 5) % 2]
                for c in range(CC):
                    last = nc.tensor.transpose(f[:, c * C:(c + 1) * C], xn[:, j, c * P:(c + 1) * P], ident)
                last.then_inc(xt_mm, 1)

            def kq(t):
                pe.wait_ge(xnT_lo, t.nth(1, 1))
                if not (isinstance(t.pair, int) and t.off < 1):
                    pe.wait_ge(mix_ev, (t + -1).nth(J, 1))
                else:
                    pe.wait_ge(w_lo, 2)
                    pe.wait_ge(xt_ev, t.nth(J, 2))
                f = f_ps[(11 * t.off) % 2]
                for j in range(J):
                    for c in range(CC):
                        last = split_mm(f[:, j * KQ:(j + 1) * KQ], cut(xnT, ALL, c, slice(j * C, (j + 1) * C)),
                                        cut(wkq, ALL, c), c == 0, c == CC - 1)
                last.then_inc(kq_mm, 1)

            def v_half(t, j, h):
                if h == 0:
                    if j == 1:
                        pe.wait_ge(kq_ev, t.nth(1, 1))
                    elif not (isinstance(t.pair, int) and t.off < 1):
                        pe.wait_ge(mix_ev, (t + -1).nth(J, 2))
                f = f_ps[(11 * t.off + 1 + j) % 2]
                for c in (2 * h, 2 * h + 1):
                    last = split_mm(f, cut(xnT, ALL, c, slice(j * C, (j + 1) * C)), cut(wv, ALL, c),
                                    c == 0, c == CC - 1)
                if h:
                    last.then_inc(v_mm, 1)

            def k_half(t, m, h):
                if h == 0:
                    if m == 0:
                        pe.wait_ge(xk_lo, t.nth(2, 2))
                        if t.off == 0:
                            pe.wait_ge(w_lo, NW)
                        pe.wait_ge(v_ev, t.nth(J, 2))
                    else:
                        pe.wait_ge(relu_ev, t.nth(2, 1))
                f = f_ps[(11 * t.off + (4 if m == 0 else 6)) % 2]
                d = 2 * m + h
                for c in range(CC):
                    last = split_mm(f[:, h * TT:(h + 1) * TT], cut(wfk, ALL, c, slice(d * P, (d + 1) * P)),
                                    cut(xkT, ALL, c), c == 0, c == CC - 1)
                if h:
                    last.then_inc(k_mm, 1)

            def r_half(t, j, h):
                if h == 0:
                    if j == 0:
                        pe.wait_ge(xr_lo, t.nth(2, 2))
                        if t.off < NT - 1:
                            pe.wait_ge(xt_ev, (t + 1).nth(J, 2))
                    else:
                        pe.wait_ge(relu_ev, t.nth(2, 2))
                f = f_ps[(11 * t.off + 7 + j) % 2]
                for c in (2 * h, 2 * h + 1):
                    last = split_mm(f, cut(xrT, ALL, c, slice(j * C, (j + 1) * C)), cut(wr, ALL, c),
                                    c == 0, c == CC - 1)
                if h:
                    last.then_inc(r_mm, 1)

            def kv_half(t, j, h):
                if h == 0:
                    pe.wait_ge(r_ev, t.nth(J, j + 1))
                    pe.wait_ge(act_lo, t.nth(2, 2))
                f = f_ps[(11 * t.off + 9 + j) % 2]
                for c in (2 * h, 2 * h + 1):
                    last = split_mm(f, cut(actT, ALL, c, slice(j * C, (j + 1) * C)), cut(wfv, ALL, c),
                                    c == 0, c == CC - 1)
                if h:
                    last.then_inc(kv_mm, 1)

            def kq_transposes(t, j):
                if j == 0:
                    pe.wait_ge(kn_lo, t.nth(1, 1))
                    pe.wait_ge(qn_lo, t.nth(1, 1))
                    if not (isinstance(t.pair, int) and t.off < 1):
                        pe.wait_ge(kp_lo, t.nth(1, 0))
                elif not (isinstance(t.pair, int) and t.off < 1):
                    pe.wait_ge(x_up, t.nth(LEVELS, 0))
                dst = (b_ps, a_ps)[j]
                rows = kn[t.par][:, j].bitcast(F32)
                nc.tensor.transpose(dst[:, 0:C], rows[:, 3 * DS:5 * DS], ident)
                nc.tensor.transpose(dst[:, C:2 * C], rows[:, DS:3 * DS], ident)
                nc.tensor.transpose(dst[:, 2 * C:3 * C], qn[:, j].bitcast(F32), ident).then_inc(kqT_mm, 1)

            def products(t):
                pe.wait_ge(kqT_ev, t.nth(J, 2))
                for j in range(J):
                    both = kqT[t.par][:, j, 1:3].rearrange("p k q -> p (k q)")
                    dst = a_ps[:, 2 * j * C:2 * (j + 1) * C]
                    mm(dst, kqT[t.par][:, j, 1], both, True, False)
                    last = mm(dst, kqT[t.par][:, j, 0], both, False, True)
                last.then_inc(g_mm, 1)

            def level(t, i):
                if i == 0:
                    pe.wait_ge(at_ev, t.nth(1, 1))
                    pe.wait_ge(mt_ev, t.nth(1, 1))
                    pe.wait_ge(m_ev, t.nth(1, 1))
                else:
                    pe.wait_ge(pt_ev, t.nth(LEVELS, i))
                    if i == 1:
                        pe.wait_ge(x0_done, t.nth(1, 1))
                    else:
                        pe.wait_ge(x_up, t.nth(LEVELS, i - 1))
                for j in range(J):
                    a, b = (0, 1) if i == 0 else (1, 2) if i == LEVELS else (0, 2)
                    last = mm(a_ps[:, (2 * j + a) * C:(2 * j + b) * C], pt[:, j],
                              px[:, j, a:b].rearrange("p k q -> p (k q)"), True, True)
                last.then_inc(lv_mm, 1)

            def level_transposes(t, i):
                pe.wait_ge(p_ev, t.nth(LEVELS, i))
                for j in range(J):
                    last = nc.tensor.transpose(b_ps[:, j * C:(j + 1) * C], px[:, j, 0], ident)
                last.then_inc(lt_mm, 1)

            def tk(p):
                pe.wait_ge(t_lo, p.nth(1, 1))
                pe.wait_ge(pt_ev, p.nth(LEVELS, LEVELS))
                for j in range(J):
                    rows = kn[p.par][:, j]
                    last = split_mm(b_ps[:, j * C:(j + 1) * C], (rows[:, 0:2 * DS], rows[:, 2 * DS:4 * DS]),
                                    cut(tT, ALL, j), True, True)
                last.then_inc(kp_mm, 1)

            def u_and_qs(p, j):
                if j == 0:
                    pe.wait_ge(kp_lo, p.nth(1, 1))
                    pe.wait_ge(v_lo, p.nth(J, 2))
                if j or not (isinstance(p.pair, int) and p.off < 1):
                    pe.wait_ge(u_lo, p.nth(J, j))
                    pe.wait_ge(sc_lo, p.nth(J, j))
                split_mm(u_ps, cut(tT, ALL, j), cut(v[p.par], ALL, j), True, False)
                mm(u_ps, kp[:, j], s_hi[p.par], False, False)
                mm(u_ps, kp[:, j], s_lo[p.par], False, True).then_inc(u_mm, 1)
                if j or not (isinstance(p.pair, int) and p.off < 1):
                    pe.wait_ge(y_add, p.nth(J, j))
                mm(y_ps, kqT[p.par][:, j, 2], s_hi[p.par], True, False)
                mm(y_ps, kqT[p.par][:, j, 2], s_lo[p.par], False, False)

            def s_and_y(p, j):
                pe.wait_ge(u_lo, p.nth(J, j + 1))
                rows = kn[p.par][:, j]
                for w, m in ((0, 0), (1, 0), (0, 1)):
                    last = nc.tensor.matmul(s_ps[p.par], rows[:, 2 * w * DS:2 * (w + 1) * DS], u[m],
                                            start=False, stop=False, skip_group_check=True)
                last.then_inc(s_mm, 1)
                pe.wait_ge(at_lo, p.nth(1, 1))
                split_mm(y_ps, cut(at[p.par], ALL, j), u, False, True).then_inc(y_mm, 1)

            def step(t, main=True, prev=True, nxt=True):
                p, n = t + -1, t + 1
                if main:
                    kq(t)
                if prev:
                    level(p, LEVELS)
                if main:
                    v_half(t, 0, 0)
                if prev:
                    tk(p)
                if main:
                    v_half(t, 0, 1)
                    kq_transposes(t, 0)
                if prev:
                    u_and_qs(p, 0)
                if main:
                    kq_transposes(t, 1)
                    v_half(t, 1, 0)
                    products(t)
                if prev:
                    s_and_y(p, 0)
                if main:
                    v_half(t, 1, 1)
                    level(t, 0)
                if nxt:
                    xn_transposes(n, 0)
                if main:
                    k_half(t, 0, 0)
                    level_transposes(t, 1)
                    k_half(t, 0, 1)
                    level(t, 1)
                if prev:
                    u_and_qs(p, 1)
                if nxt:
                    xn_transposes(n, 1)
                if main:
                    level_transposes(t, 2)
                    k_half(t, 1, 0)
                    level(t, 2)
                if prev:
                    s_and_y(p, 1)
                if main:
                    k_half(t, 1, 1)
                    level_transposes(t, 3)
                    r_half(t, 0, 0)
                    level(t, 3)
                    r_half(t, 0, 1)
                    level_transposes(t, 4)
                    r_half(t, 1, 0)
                    level(t, 4)
                    r_half(t, 1, 1)
                    level_transposes(t, 5)
                    kv_half(t, 0, 0)
                    level(t, 5)
                    kv_half(t, 0, 1)
                    level_transposes(t, 6)
                    kv_half(t, 1, 0)
                    kv_half(t, 1, 1)

            pe.wait_ge(consts, 1)
            for j in range(J):
                xn_transposes(Tile(0, 0), j)
            step(Tile(0, 0), prev=False)
            with pe.Fori(0, PAIRS) as i:
                for b in range(2):
                    step(Tile(i, 1 + b))
            step(Tile(0, NT - 1), nxt=False)
            step(Tile(0, NT), main=False, nxt=False)


def kernel(L0_attn_x, L0_attn_Wk, L0_attn_bk, L0_attn_Wv, L0_attn_bv, L0_attn_Wq, L0_attn_bq, L0_attn_gamma,
           L0_attn_beta, L0_ffn_W_r, L0_ffn_W_k, L0_ffn_W_v, L0_ffn_mu_r, L0_ffn_mu_k):
    import numpy as np
    import concourse.bacc as bacc
    from concourse.bass_utils import run_bass_kernel_spmd

    def by_channel(a):
        return np.transpose(np.reshape(a, (-1, 128)))

    arrays = {
        "x": L0_attn_x, "Wk_t": np.transpose(L0_attn_Wk), "bk": L0_attn_bk, "Wv_t": np.transpose(L0_attn_Wv),
        "bv": L0_attn_bv, "Wq_t": np.transpose(L0_attn_Wq), "bq": L0_attn_bq, "gamma": by_channel(L0_attn_gamma),
        "beta": by_channel(L0_attn_beta), "Wr_t": np.transpose(L0_ffn_W_r), "Wfk_t": np.transpose(L0_ffn_W_k),
        "Wfv_t": np.transpose(L0_ffn_W_v), "mu_r": by_channel(L0_ffn_mu_r), "mu_k": by_channel(L0_ffn_mu_k),
    }
    arrays = {name: np.ascontiguousarray(a) for name, a in arrays.items()}
    nc = bacc.Bacc("TRN2", target_bir_lowering=False, num_devices=1)
    args = [nc.dram_tensor(name, a.shape, mybir.dt.from_np(a.dtype), kind="ExternalInput").ap()
            for name, a in arrays.items()]
    out = nc.dram_tensor("out", arrays["x"].shape, F32, kind="ExternalOutput").ap()
    build(nc, *args, out)
    result = run_bass_kernel_spmd(nc, [arrays], core_ids=[0])
    return result.results[0]["out"]
```

```python
from contextlib import ExitStack

import concourse.bass as bass
from concourse import mybir

F32 = mybir.dt.float32
F32R = mybir.dt.float32r
BF16 = mybir.dt.bfloat16
ALU = mybir.AluOpType
ACT = mybir.ActivationFunctionType

LR = 0.01
EPS = 1e-5


class Tile:

    def __init__(self, pair, off):
        self.pair, self.off = pair, off
        self.par = off % 2

    def __add__(self, n):
        return Tile(self.pair, self.off + n)

    def nth(self, per, k):
        n = per * self.off + k
        return n if isinstance(self.pair, int) else self.pair * (2 * per) + n

    def pos(self):
        return self.off // 2 if isinstance(self.pair, int) else self.pair + self.off // 2


def build(nc, x, Wk_t, bk, Wv_t, bv, Wq_t, bq, gamma, beta, Wr_t, Wfk_t, Wfv_t, mu_r, mu_k, out):
    P = 128
    B, S, D = x.shape
    DS = Wk_t.shape[1]
    KQ = 2 * DS
    CC = D // P
    C = P
    J = 2
    TT = J * C
    assert B == 2 and KQ == P
    NT = B * S // TT
    LEVELS = 6
    assert 2 ** (LEVELS + 1) == C

    x_v = x.rearrange("b (n q) d -> b n q d", q=TT)
    out_v = out.rearrange("b (n q) d -> b n q d", q=C)

    def w_view(w):
        return w.rearrange("(c p) n -> p c n", p=P)

    ctx = ExitStack()
    with ctx:
        def sb(name, shape, dt=F32):
            return ctx.enter_context(nc.sbuf_tensor(name, shape, dt))[:]

        def pb(name):
            return ctx.enter_context(nc.psum_tensor(name, [P, 512], F32))[:]

        def sem(name):
            return ctx.enter_context(nc.semaphore(name))

        def halves(name, shape):
            return sb(name + "_hi", shape, F32R), sb(name + "_lo", shape, F32R)

        wkq = halves("wkq", [P, CC, KQ])
        wv = halves("wv", [P, CC, D])
        wr = halves("wr", [P, CC, D])
        wfk = halves("wfk", [P, CC, D])
        wfv = halves("wfv", [P, CC, D])
        cols = sb("cols", [P, 4, CC])
        bias_v = sb("bias_v", [P, D])
        bias_kq = sb("bias_kq", [P, KQ])
        ident = sb("ident", [P, P])
        upper = sb("upper", [P, P], BF16)
        lower_lr = sb("lower_lr", [P, P])
        pair_lr = sb("pair_lr", [P, P])
        couple = sb("couple", [P, LEVELS, C // 2], BF16)
        spare = sb("spare", [P, 1])
        small = sb("small", [P, 4, J])
        ones = sb("ones", [P, 4, J])

        x_in = sb("x_in", [P, J, D])
        bn = sb("bn", [P, J, 6])
        mv = sb("mv", [P, J, 2])
        st = sb("st", [P, 4, J])
        st_tmp = sb("st_tmp", [P, 4, J])
        st_keep = [sb(f"st_keep{i}", [P, 4, J]) for i in range(2)]
        xn = sb("xn", [P, J, D])
        xt = sb("xt", [P, CC, TT + 1])
        carry = [sb(f"carry{i}", [P, CC, 1]) for i in range(2)]
        dx = sb("dx", [P, CC, TT])
        mix = sb("mix", [P, CC // 2, TT])
        xnT = halves("xnT", [P, CC, TT])
        xkT = halves("xkT", [P, CC, TT])
        xrT = halves("xrT", [P, CC, TT])

        kq32 = sb("kq32", [P, J, KQ])
        kn = [sb(f"kn{i}", [P, J, 5 * DS], F32R) for i in range(2)]
        qn = sb("qn", [P, J, 2 * DS], F32R)
        kqT = [sb(f"kqT{i}", [P, J, 3, C], F32R) for i in range(2)]
        v32 = sb("v32", [P, J, D])
        v = [halves(f"v{i}", [P, J, D]) for i in range(2)]
        at32 = kq32
        beta_b = v32[:, 0].rearrange("p (c q) -> p c q", c=CC)
        at = [halves(f"at{i}", [P, J, C]) for i in range(2)]
        mt = sb("mt", [P, J, C])
        xi = sb("xi", [P, J, C])
        xiT = sb("xiT", [P, J, C])
        ox = sb("ox", [P, J, C // 2])
        tT = halves("tT", [P, J, C])
        kp = sb("kp", [P, J, C], F32R)
        act32 = sb("act32", [P, CC, TT])
        actT = halves("actT", [P, CC, TT])
        gate_r = sb("gate_r", [P, J, D])
        g = sb("g", [P, 2, J, D])

        s_hi = [sb(f"s_hi{i}", [P, D], F32R) for i in range(2)]
        s_lo = [sb(f"s_lo{i}", [P, D], F32R) for i in range(2)]
        u = halves("u", [P, D])
        x_res = sb("x_res", [P, 2, J, D])
        o = sb("o", [P, J, D])

        s_ps = [pb(f"s_ps{i}") for i in range(2)]
        u_ps = pb("u_ps")
        y_ps = pb("y_ps")
        f_ps = [pb(f"f_ps{i}") for i in range(2)]
        a_ps = pb("a_ps")
        b_ps = pb("b_ps")

        cols_ld = sem("cols_ld")
        bias_ld = sem("bias_ld")
        w_ld = [sem(f"w_ld{i}") for i in range(2)]
        x_ld = sem("x_ld")
        xres_ld = [sem(f"xres_ld{i}") for i in range(2)]
        out_st = [sem(f"out_st{i}") for i in range(J)]
        const0 = sem("const0")
        couple0 = sem("couple0")
        consts = sem("consts")
        dve_zero = sem("dve_zero")
        s_zero = sem("s_zero")
        beta_bc = sem("beta_bc")
        bias_mm = sem("bias_mm")
        bias_add = sem("bias_add")
        bias_done = sem("bias_done")
        w_fold = sem("w_fold")
        w_hi = sem("w_hi")
        w_lo = sem("w_lo")
        bn_done = sem("bn_done")
        mv_done = sem("mv_done")
        st_step = sem("st_step")
        st_done = sem("st_done")
        kept = sem("kept")
        xn_done = sem("xn_done")
        xt_mm = sem("xt_mm")
        carried = sem("carried")
        xt_first = sem("xt_first")
        xt_ev = sem("xt_ev")
        xnT_hi = sem("xnT_hi")
        xnT_lo = sem("xnT_lo")
        dx_done = sem("dx_done")
        xk_mix = sem("xk_mix")
        xk_hi = sem("xk_hi")
        xk_lo = sem("xk_lo")
        xr_mix = sem("xr_mix")
        xr_hi = sem("xr_hi")
        xr_lo = sem("xr_lo")
        kq_mm = sem("kq_mm")
        kq_ev = sem("kq_ev")
        kn_hi = sem("kn_hi")
        kn_lo = sem("kn_lo")
        qn_hi = sem("qn_hi")
        qn_lo = sem("qn_lo")
        kqT_mm = sem("kqT_mm")
        kqT_ev = sem("kqT_ev")
        g_mm = sem("g_mm")
        mt_ev = sem("mt_ev")
        pair_ev = sem("pair_ev")
        x0_done = sem("x0_done")
        at_ev = sem("at_ev")
        at_hi = sem("at_hi")
        at_lo = sem("at_lo")
        xT_mm = sem("xT_mm")
        ox_mm = sem("ox_mm")
        xox_mm = sem("xox_mm")
        ox_ev = sem("ox_ev")
        xT_ev = sem("xT_ev")
        x_up = sem("x_up")
        t_hi = sem("t_hi")
        t_lo = sem("t_lo")
        kp_mm = sem("kp_mm")
        kp_hi = sem("kp_hi")
        kp_lo = sem("kp_lo")
        v_mm = sem("v_mm")
        v_ev = sem("v_ev")
        v_hi = sem("v_hi")
        v_lo = sem("v_lo")
        k_mm = sem("k_mm")
        relu_ev = sem("relu_ev")
        square = sem("square")
        act_hi = sem("act_hi")
        act_lo = sem("act_lo")
        r_mm = sem("r_mm")
        r_ev = sem("r_ev")
        kv_mm = sem("kv_mm")
        mix_ev = sem("mix_ev")
        sig = sem("sig")
        g_done = sem("g_done")
        u_mm = sem("u_mm")
        u_hi = sem("u_hi")
        u_lo = sem("u_lo")
        s_mm = sem("s_mm")
        sc_hi = sem("sc_hi")
        sc_lo = sem("sc_lo")
        y_mm = sem("y_mm")
        xn_again = sem("xn_again")
        y_add = sem("y_add")
        gated = sem("gated")
        o_done = sem("o_done")

        stage = [x_res[:, :, :, :].rearrange("p a j d -> p (a j) d"),
                 g[:, :, :, :].rearrange("p a j d -> p (a j) d")]
        WEIGHTS = [(wkq, KQ), (wv, D), (wfk, D), (wr, D), (wfv, D)]
        NW = len(WEIGHTS)

        def staged(n):
            return stage[n % 2][:, :, 0:WEIGHTS[n][1]]

        def w_count(n):
            return 16 * (n // 2 + 1) + (16 if n % 2 == 0 else 0)

        FIRST = 3
        PAIRS = (NT - 1 - FIRST) // 2

        def second_halves(m, i):
            return m.rearrange("p j (n h b) -> p j n h b", h=2, b=2 ** i)[:, :, :, 1]

        SECOND = {"v0", "k0", "xt1", "r0", "mix0"}

        def bank(t, what):
            return f_ps[(t.par + (what in SECOND)) % 2]

        block = ctx.enter_context(nc.Block())

        @block.sync
        def _(sp):
            def load_x(n):
                if not (isinstance(n.pair, int) and n.off < 1):
                    sp.wait_ge(xn_done, n.nth(1, 0))
                sp.dma_start(x_in, x_v[n.par, bass.ds(n.pos(), 1), :, :].rearrange(
                    "a (j q) d -> q (a j) d", q=C)).then_inc(x_ld, 16)

            def load_x_res(t):
                if isinstance(t.pair, int) and t.off < 2:
                    sp.wait_ge(w_lo, NW)
                else:
                    sp.wait_ge(o_done, (t + -1).nth(J, 0))
                sp.dma_start(x_res[:, t.par], x_v[t.par, bass.ds(t.pos(), 1), :, :].rearrange(
                    "a (j q) d -> q (a j) d", q=C)).then_inc(xres_ld[t.par], 16)

            def store(p, j):
                sp.wait_ge(o_done, p.nth(J, j + 1))
                sp.dma_start(out_v[p.par, bass.ds(p.pos() * J + j, 1), :, :].rearrange("a q d -> q (a d)"),
                             o[:, j]).then_inc(out_st[j], 16)

            def step(t, main=True, prev=True, ahead=True):
                if ahead:
                    load_x(t + 1)
                if main:
                    load_x_res(t)
                if prev:
                    for j in range(J):
                        store(t + -1, j)

            load_x(Tile(0, 0))
            for n, w in enumerate(((Wk_t, Wq_t), Wv_t, Wfk_t, Wr_t, Wfv_t)):
                if n >= 2:
                    sp.wait_ge(w_lo, n - 1)
                if n == 0:
                    for i, part in enumerate(w):
                        sp.dma_start(staged(0)[:, :, i * DS:(i + 1) * DS], w_view(part)).then_inc(w_ld[0], 16)
                else:
                    sp.dma_start(staged(n), w_view(w)).then_inc(w_ld[n % 2], 16)
            step(Tile(0, 0), prev=False)
            for t in range(1, FIRST):
                step(Tile(0, t))
            with sp.Fori(0, PAIRS) as i:
                for b in range(2):
                    step(Tile(i, FIRST + b))
            step(Tile(0, NT - 1), ahead=False)
            step(Tile(0, NT), main=False, ahead=False)
            for j in range(J):
                sp.wait_ge(out_st[j], 16 * NT)

        @block.gpsimd
        def _(pool):
            nc.gpsimd.memset(ident, 0.0)
            nc.gpsimd.memset(upper, 1.0)
            nc.gpsimd.memset(lower_lr, -LR)
            nc.gpsimd.memset(pair_lr, 0.0)
            nc.gpsimd.memset(couple, 1.0)
            for k, value in enumerate((EPS, LR, -0.5, 1.0)):
                nc.gpsimd.memset(small[:, k], value)
            nc.gpsimd.memset(ones, 1.0).then_inc(const0, 1)
            pool.wait_ge(const0, 1)
            nc.gpsimd.affine_select(out=ident, in_=ident, compare_op=ALU.not_equal, fill=1.0, base=0,
                                    pattern=[[-1, P]], channel_multiplier=1)
            nc.gpsimd.affine_select(out=upper, in_=upper, compare_op=ALU.is_gt, fill=0.0, base=0,
                                    pattern=[[1, P]], channel_multiplier=-1)
            nc.gpsimd.affine_select(out=lower_lr, in_=lower_lr, compare_op=ALU.is_gt, fill=0.0, base=0,
                                    pattern=[[-1, P]], channel_multiplier=1)
            even = pair_lr.rearrange("p (n h) -> p n h", h=2)[:, :, 1]
            nc.gpsimd.affine_select(out=even, in_=even, compare_op=ALU.not_equal, fill=-LR, base=0,
                                    pattern=[[-2, P // 2]], channel_multiplier=1)
            for i in range(1, LEVELS + 1):
                b = 2 ** i
                m = couple[:, i - 1].rearrange("p (n b) -> p n b", b=b)
                nc.gpsimd.affine_select(out=m, in_=m, compare_op=ALU.is_ge, fill=0.0, base=0,
                                        pattern=[[-2 * b, C // (2 * b)], [0, b]],
                                        channel_multiplier=1).then_inc(couple0, 1)
            for i in range(1, LEVELS + 1):
                b = 2 ** i
                m = couple[:, i - 1].rearrange("p (n b) -> p n b", b=b)
                pool.wait_ge(couple0, i)
                last = nc.gpsimd.affine_select(out=m, in_=m, compare_op=ALU.is_ge, fill=0.0, base=b - 1,
                                               pattern=[[2 * b, C // (2 * b)], [0, b]],
                                               channel_multiplier=-1)
            last.then_inc(consts, 1)
            pool.wait_ge(consts, 1)

            def norm_scalars(n):
                steps = 7
                mean, var = mv[:, :, 0], mv[:, :, 1]
                eps, lr, power, one = (small[:, k] for k in range(4))
                pool.wait_ge(mv_done, n.nth(1, 1))
                if not (isinstance(n.pair, int) and n.off < 1):
                    pool.wait_ge(kept, n.nth(1, 0))
                    pool.wait_ge(xn_done, n.nth(1, 0))
                nc.gpsimd.tensor_tensor(st[:, 0], mean, one, ALU.mult).then_inc(st_step, 1)
                nc.gpsimd.tensor_tensor(st_tmp[:, 0], var, eps, ALU.add).then_inc(st_step, 1)
                pool.wait_ge(st_step, n.nth(steps, 2))
                nc.gpsimd.tensor_tensor(st[:, 1], st_tmp[:, 0], power, ALU.pow).then_inc(st_step, 1)
                pool.wait_ge(st_step, n.nth(steps, 3))
                nc.gpsimd.tensor_tensor(st_tmp[:, 1], st[:, 1], st[:, 1], ALU.mult).then_inc(st_step, 1)
                pool.wait_ge(st_step, n.nth(steps, 4))
                nc.gpsimd.tensor_tensor(st_tmp[:, 2], st_tmp[:, 1], var, ALU.mult).then_inc(st_step, 1)
                pool.wait_ge(st_step, n.nth(steps, 5))
                nc.gpsimd.tensor_tensor(st_tmp[:, 3], st_tmp[:, 2], eps, ALU.add).then_inc(st_step, 1)
                pool.wait_ge(st_step, n.nth(steps, 6))
                nc.gpsimd.tensor_tensor(st[:, 2], st_tmp[:, 3], power, ALU.pow).then_inc(st_step, 1)
                pool.wait_ge(st_step, n.nth(steps, 7))
                nc.gpsimd.tensor_tensor(st[:, 3], st[:, 2], lr, ALU.mult).then_inc(st_done, 1)

            def shift_difference(n):
                pool.wait_ge(xt_ev, n.nth(J, 2))
                pool.wait_ge(xt_first, n.nth(1, 1))
                if not (isinstance(n.pair, int) and n.off < 1):
                    pool.wait_ge(xr_mix, n.nth(2, 0))
                nc.gpsimd.tensor_tensor(dx, xt[:, :, 1:TT + 1], xt[:, :, 0:TT], ALU.subtract).then_inc(dx_done, 1)

            def keep_scalars(t):
                if not (isinstance(t.pair, int) and t.off < 2):
                    pool.wait_ge(xn_again, (t + -1).nth(J, 0))
                pool.wait_ge(st_done, t.nth(1, 1))
                nc.gpsimd.tensor_tensor(st_keep[t.par], st, ones, ALU.mult).then_inc(kept, 1)

            def v_low(t, j):
                pool.wait_ge(v_hi, t.nth(J, j + 1))
                nc.gpsimd.tensor_tensor(v[t.par][1][:, j], v32[:, j], v[t.par][0][:, j].bitcast(F32),
                                        ALU.subtract).then_inc(v_lo, 1)

            def at_low(t):
                pool.wait_ge(at_hi, t.nth(1, 1))
                nc.gpsimd.tensor_tensor(at[t.par][1], at32, at[t.par][0].bitcast(F32),
                                        ALU.subtract).then_inc(at_lo, 1)

            def act_low(t, m):
                half = slice(m * CC // 2, (m + 1) * CC // 2)
                pool.wait_ge(act_hi, t.nth(2, m + 1))
                if not (isinstance(t.pair, int) and t.off < 1):
                    pool.wait_ge(kv_mm, t.nth(J, 0))
                nc.gpsimd.tensor_tensor(actT[1][:, half], act32[:, half], actT[0][:, half].bitcast(F32),
                                        ALU.subtract).then_inc(act_lo, 1)

            def silu(t, j):
                pool.wait_ge(sig, t.nth(J, j + 1))
                nc.gpsimd.tensor_tensor(g[:, t.par, j], g[:, t.par, j], gate_r[:, j], ALU.mult).then_inc(g_done, 1)

            def output(p, j):
                pool.wait_ge(y_add, p.nth(J, j + 1))
                pool.wait_ge(g_done, p.nth(J, j + 1))
                nc.gpsimd.tensor_tensor(o[:, j], o[:, j], g[:, p.par, j], ALU.mult).then_inc(gated, 1)
                pool.wait_ge(gated, p.nth(J, j + 1))
                nc.gpsimd.tensor_tensor(o[:, j], o[:, j], x_res[:, p.par, j], ALU.add).then_inc(o_done, 1)

            def step(t, main=True, prev=True, nxt=True):
                p, n = t + -1, t + 1
                if main:
                    keep_scalars(t)
                    v_low(t, 0)
                if nxt:
                    norm_scalars(n)
                if main:
                    v_low(t, 1)
                    at_low(t)
                if prev:
                    output(p, 0)
                if main:
                    act_low(t, 0)
                if nxt:
                    shift_difference(n)
                if main:
                    act_low(t, 1)
                if prev:
                    output(p, 1)
                if main:
                    silu(t, 0)
                    silu(t, 1)

            norm_scalars(Tile(0, 0))
            shift_difference(Tile(0, 0))
            step(Tile(0, 0), prev=False)
            for t in range(1, FIRST):
                step(Tile(0, t))
            with pool.Fori(0, PAIRS) as i:
                for b in range(2):
                    step(Tile(i, FIRST + b))
            step(Tile(0, NT - 1), nxt=False)
            step(Tile(0, NT), main=False, nxt=False)

        @block.scalar
        def _(act):
            act.dma_start(cols[:, 0], gamma).then_inc(cols_ld, 16)
            act.dma_start(cols[:, 1], beta).then_inc(cols_ld, 16)
            act.dma_start(cols[:, 2], mu_r).then_inc(cols_ld, 16)
            act.dma_start(cols[:, 3], mu_k).then_inc(cols_ld, 16)
            act.dma_start(bias_v, bv.partition_broadcast(P)).then_inc(bias_ld, 16)
            act.dma_start(bias_kq[:, 0:DS], bk.partition_broadcast(P)).then_inc(bias_ld, 16)
            act.dma_start(bias_kq[:, DS:KQ], bq.partition_broadcast(P)).then_inc(bias_ld, 16)

            def copy(out_, in_, **kw):
                return nc.scalar.activation(out_, in_, ACT.Copy, **kw)

            for n in range(NW):
                if n < 2:
                    act.wait_ge(w_fold, n + 1)
                else:
                    act.wait_ge(w_ld[n % 2], w_count(n))
                copy(WEIGHTS[n][0][0], staged(n)).then_inc(w_hi, 1)

            def transposed(n, j):
                act.wait_ge(xt_mm, n.nth(J, j + 1))
                if j == 0 and not (isinstance(n.pair, int) and n.off < 1):
                    act.wait_ge(carried, n.nth(1, 0))
                    act.wait_ge(xr_mix, n.nth(2, 0))
                    act.wait_ge(xnT_lo, n.nth(1, 0))
                f = bank(n + -1, f"xt{j}")
                copy(xt[:, :, 1 + j * C:1 + (j + 1) * C],
                     f.rearrange("p (c q) -> p c q", c=CC)).then_inc(xt_ev, 1)

            def xn_high(n):
                act.wait_ge(xt_ev, n.nth(J, 2))
                if not (isinstance(n.pair, int) and n.off < 1):
                    act.wait_ge(v_mm, n.nth(J, 0))
                copy(xnT[0], xt[:, :, 1:TT + 1]).then_inc(xnT_hi, 1)

            def kqT_copy(t, j):
                act.wait_ge(kqT_mm, t.nth(J, j + 1))
                src = (b_ps, a_ps)[j]
                copy(kqT[t.par][:, j], src[:, 0:3 * C].rearrange("p (k q) -> p k q", k=3)).then_inc(kqT_ev, 1)

            def v_high(t, j):
                act.wait_ge(v_ev, t.nth(J, j + 1))
                copy(v[t.par][0][:, j], v32[:, j]).then_inc(v_hi, 1)

            def at_high(t):
                act.wait_ge(at_ev, t.nth(1, 1))
                copy(at[t.par][0], at32).then_inc(at_hi, 1)

            def x_transposed(t, i):
                act.wait_ge(xT_mm, t.nth(LEVELS, i))
                copy(xiT, b_ps[:, 0:J * C].rearrange("p (j q) -> p j q", j=J)).then_inc(xT_ev, 1)

            def t_high(p):
                act.wait_ge(x_up, p.nth(LEVELS, LEVELS))
                if not (isinstance(p.pair, int) and p.off < 1):
                    act.wait_ge(u_mm, p.nth(J, 0))
                copy(tT[0], xi).then_inc(t_hi, 1)

            def kp_high(p):
                act.wait_ge(kp_mm, p.nth(1, 1))
                copy(kp, b_ps[:, 0:J * C].rearrange("p (j q) -> p j q", j=J), scale=-LR).then_inc(kp_hi, 1)

            def u_high(p, j):
                act.wait_ge(u_mm, p.nth(J, j + 1))
                if j or not (isinstance(p.pair, int) and p.off < 1):
                    act.wait_ge(y_mm, p.nth(J, j))
                copy(u[0], u_ps).then_inc(u_hi, 1)

            def s_high(p, j):
                act.wait_ge(s_mm, p.nth(J, j + 1))
                copy(s_hi[p.par], s_ps[p.par]).then_inc(sc_hi, 1)

            def relu(t, m):
                act.wait_ge(k_mm, t.nth(2, m + 1))
                if not (isinstance(t.pair, int) and t.off < 1):
                    act.wait_ge(act_lo, t.nth(2, 0))
                nc.scalar.activation(act32[:, 2 * m:2 * m + 2], bank(t, f"k{m}").rearrange("p (c q) -> p c q", c=2), ACT.Relu).then_inc(relu_ev, 1)

            def act_high(t, m):
                act.wait_ge(square, t.nth(2, m + 1))
                if not (isinstance(t.pair, int) and t.off < 1):
                    act.wait_ge(kv_mm, t.nth(J, 0))
                copy(actT[0][:, 2 * m:2 * m + 2], act32[:, 2 * m:2 * m + 2]).then_inc(act_hi, 1)

            def sigmoid_r(t, j):
                act.wait_ge(r_mm, t.nth(J, j + 1))
                if not (isinstance(t.pair, int) and t.off < 1):
                    act.wait_ge(g_done, t.nth(J, 0))
                nc.scalar.activation(gate_r[:, j], bank(t, f"r{j}"), ACT.Sigmoid).then_inc(r_ev, 1)

            def sigmoid_mix(t, j):
                act.wait_ge(mix_ev, t.nth(J, j + 1))
                nc.scalar.activation(gate_r[:, j], g[:, t.par, j], ACT.Sigmoid).then_inc(sig, 1)

            def step(t, main=True, prev=True, nxt=True):
                p, n = t + -1, t + 1
                if prev:
                    t_high(p)
                if main:
                    v_high(t, 0)
                    kqT_copy(t, 0)
                    kqT_copy(t, 1)
                if prev:
                    kp_high(p)
                if main:
                    at_high(t)
                    v_high(t, 1)
                if prev:
                    u_high(p, 0)
                if main:
                    x_transposed(t, 1)
                if prev:
                    s_high(p, 0)
                if nxt:
                    transposed(n, 0)
                if main:
                    relu(t, 0)
                    x_transposed(t, 2)
                    act_high(t, 0)
                if nxt:
                    transposed(n, 1)
                if prev:
                    u_high(p, 1)
                if main:
                    relu(t, 1)
                    x_transposed(t, 3)
                if prev:
                    s_high(p, 1)
                if nxt:
                    xn_high(n)
                if main:
                    act_high(t, 1)
                    x_transposed(t, 4)
                    sigmoid_r(t, 0)
                    x_transposed(t, 5)
                    sigmoid_r(t, 1)
                    x_transposed(t, 6)
                    sigmoid_mix(t, 0)
                    sigmoid_mix(t, 1)

            for j in range(J):
                transposed(Tile(0, 0), j)
            xn_high(Tile(0, 0))
            step(Tile(0, 0), prev=False)
            for t in range(1, FIRST):
                step(Tile(0, t))
            with act.Fori(0, PAIRS) as i:
                for b in range(2):
                    step(Tile(i, FIRST + b))
            step(Tile(0, NT - 1), nxt=False)
            step(Tile(0, NT), main=False, nxt=False)

        @block.vector
        def _(dve):
            V = nc.vector

            def rounded(out_, in_):
                return V.tensor_copy(out_, in_)

            def rest(out_, in_, hi):
                return V.tensor_tensor(out_, in_, hi.bitcast(F32), ALU.subtract)

            for i in range(2):
                V.memset(s_hi[i].bitcast(F32), 0.0)
                V.memset(s_lo[i].bitcast(F32), 0.0)
                V.memset(carry[i], 0.0)
            V.memset(xt[:, :, 0:1], 0.0).then_inc(dve_zero, 1)
            dve.wait_ge(cols_ld, 64)
            V.tensor_copy(beta_b, cols[:, 1].unsqueeze(2).to_broadcast([P, CC, P])).then_inc(beta_bc, 1)
            dve.wait_ge(bias_ld, 48)
            for n, bias in ((0, bias_kq), (1, bias_v)):
                wide = WEIGHTS[n][1]
                dve.wait_ge(bias_mm, n + 1)
                V.tensor_tensor(bias, f_ps[n][:, 0:wide], bias, ALU.add).then_inc(bias_add, 1)
                for c in range(CC):
                    last = V.tensor_scalar(staged(n)[:, c], staged(n)[:, c], cols[:, 0, c:c + 1], None, ALU.mult)
                last.then_inc(w_fold, 1)
            dve.wait_ge(bias_add, 2)
            V.tensor_scalar(bias_v, bias_v, LR, None, ALU.mult).then_inc(bias_done, 1)
            for n in range(NW):
                dve.wait_ge(w_hi, n + 1)
                rest(WEIGHTS[n][0][1], staged(n), WEIGHTS[n][0][0]).then_inc(w_lo, 1)

            def stats(n):
                dve.wait_ge(x_ld, n.nth(16, 16))
                for j in range(J):
                    last = V.bn_stats(bn[:, j], x_in[:, j])
                last.then_inc(bn_done, 1)
                if not (isinstance(n.pair, int) and n.off < 1):
                    dve.wait_ge(st_done, n.nth(1, 0))
                dve.wait_ge(bn_done, n.nth(1, 1))
                V.memset(spare, 0.0)
                for j in range(J):
                    last = V.bn_aggr(mv[:, j], bn[:, j])
                last.then_inc(mv_done, 1)

            def normalise(n):
                dve.wait_ge(st_done, n.nth(1, 1))
                if not (isinstance(n.pair, int) and n.off < 1):
                    dve.wait_ge(xt_mm, n.nth(J, 0))
                for j in range(J):
                    last = V.tensor_scalar(xn[:, j], x_in[:, j], st[:, 0, j:j + 1], st[:, 1, j:j + 1],
                                           ALU.subtract, ALU.mult)
                last.then_inc(xn_done, 1)

            def carry_over(n):
                before = n + -1
                dve.wait_ge(xt_ev, before.nth(J, 2))
                V.tensor_copy(carry[before.par], xt[:, :, TT:TT + 1]).then_inc(carried, 1)

            def first_column(n):
                if not (isinstance(n.pair, int) and n.off < 1):
                    dve.wait_ge(carried, n.nth(1, 0))
                    dve.wait_ge(dx_done, n.nth(1, 0))
                    dve.wait_ge(xr_mix, n.nth(2, 0))
                V.tensor_copy(xt[:, :, 0:1], carry[n.par]).then_inc(xt_first, 1)

            def xn_low(n):
                dve.wait_ge(xnT_hi, n.nth(1, 1))
                rest(xnT[1], xt[:, :, 1:TT + 1], xnT[0]).then_inc(xnT_lo, 1)

            def mixed(n, m, dst, mu, made, hi, lo):
                for i in range(CC // 2):
                    c = m * (CC // 2) + i
                    last = V.scalar_tensor_tensor(mix[:, i], dx[:, c], cols[:, mu, c:c + 1], xt[:, c, 0:TT],
                                                  ALU.mult, ALU.add)
                last.then_inc(made, 1)
                part = slice(m * (CC // 2), (m + 1) * (CC // 2))
                dve.wait_ge(made, n.nth(2, m + 1))
                rounded(dst[0][:, part], mix).then_inc(hi, 1)
                dve.wait_ge(hi, n.nth(2, m + 1))
                rest(dst[1][:, part], mix, dst[0][:, part]).then_inc(lo, 1)

            def key_mix(n, m):
                if m:
                    dve.wait_ge(xk_lo, n.nth(2, 1))
                else:
                    dve.wait_ge(dx_done, n.nth(1, 1))
                    dve.wait_ge(xt_first, n.nth(1, 1))
                    if not (isinstance(n.pair, int) and n.off < 1):
                        dve.wait_ge(k_mm, n.nth(2, 0))
                mixed(n, m, xkT, 3, xk_mix, xk_hi, xk_lo)

            def gate_mix(n, m):
                if m:
                    dve.wait_ge(xr_lo, n.nth(2, 1))
                else:
                    dve.wait_ge(xk_lo, n.nth(2, 2))
                    if not (isinstance(n.pair, int) and n.off < 1):
                        dve.wait_ge(r_mm, n.nth(J, 0))
                mixed(n, m, xrT, 2, xr_mix, xr_hi, xr_lo)

            def kq_rows(t):
                dve.wait_ge(kq_mm, t.nth(1, 1))
                dve.wait_ge(kept, t.nth(1, 1))
                if not (isinstance(t.pair, int) and t.off < 1):
                    dve.wait_ge(at_lo, t.nth(1, 0))
                f = bank(t, "kq")
                for j in range(J):
                    last = V.scalar_tensor_tensor(kq32[:, j], f[:, j * KQ:(j + 1) * KQ], st_keep[t.par][:, 2, j:j + 1],
                                                  bias_kq, ALU.mult, ALU.add)
                last.then_inc(kq_ev, 1)
                dve.wait_ge(kq_ev, t.nth(1, 1))
                rows = kn[t.par].rearrange("p j (b e) -> p j b e", e=DS)
                for j in range(J):
                    k32 = kq32[:, j, 0:DS].unsqueeze(1).to_broadcast([P, 2, DS])
                    last = rounded(rows[:, j, 0:2], k32)
                rounded(rows[:, :, 4], kq32[:, :, 0:DS]).then_inc(kn_hi, 1)
                rounded(qn[:, :, 0:DS], kq32[:, :, DS:KQ]).then_inc(qn_hi, 1)
                dve.wait_ge(kn_hi, t.nth(1, 1))
                for j in range(J):
                    k32 = kq32[:, j, 0:DS].unsqueeze(1).to_broadcast([P, 2, DS])
                    last = rest(rows[:, j, 2:4], k32, rows[:, j, 0:2])
                last.then_inc(kn_lo, 1)
                dve.wait_ge(qn_hi, t.nth(1, 1))
                rest(qn[:, :, DS:KQ], kq32[:, :, DS:KQ], qn[:, :, 0:DS]).then_inc(qn_lo, 1)

            def v_rows(t, j):
                dve.wait_ge(v_mm, t.nth(J, j + 1))
                if not (isinstance(t.pair, int) and t.off < 1):
                    dve.wait_ge(v_lo, t.nth(J, 0))
                V.scalar_tensor_tensor(v32[:, j], bank(t, f"v{j}"), st_keep[t.par][:, 3, j:j + 1],
                                       bias_v, ALU.mult, ALU.add).then_inc(v_ev, 1)

            def masked(t):
                dve.wait_ge(g_mm, t.nth(1, 1))
                src = a_ps.rearrange("p (j k q) -> p j k q", j=J, k=2)
                if not (isinstance(t.pair, int) and t.off < 1):
                    dve.wait_ge(t_lo, t.nth(1, 0))
                V.tensor_tensor(mt, src[:, :, 0], lower_lr.unsqueeze(1).to_broadcast([P, J, C]),
                                ALU.mult).then_inc(mt_ev, 1)
                V.tensor_tensor(xi, src[:, :, 0], pair_lr.unsqueeze(1).to_broadcast([P, J, C]),
                                ALU.mult).then_inc(pair_ev, 1)
                V.tensor_tensor(at32, src[:, :, 1], upper.unsqueeze(1).to_broadcast([P, J, C]),
                                ALU.mult).then_inc(at_ev, 1)
                dve.wait_ge(pair_ev, t.nth(1, 1))
                V.tensor_tensor(xi, xi, ident.unsqueeze(1).to_broadcast([P, J, C]), ALU.add).then_inc(x0_done, 1)

            def coupled(t, i):
                dve.wait_ge(ox_mm, t.nth(LEVELS, i))
                V.tensor_tensor(ox, a_ps[:, 0:J * C // 2].rearrange("p (j q) -> p j q", j=J),
                                couple[:, i - 1].unsqueeze(1).to_broadcast([P, J, C // 2]),
                                ALU.mult).then_inc(ox_ev, 1)

            def doubled(t, i):
                dve.wait_ge(xox_mm, t.nth(LEVELS, i))
                for j in range(J):
                    dst = second_halves(xi, i)[:, j]
                    last = V.tensor_tensor(dst, a_ps[:, (J + j) * C // 2:(J + j + 1) * C // 2].rearrange(
                        "p (n b) -> p n b", b=2 ** i), dst, ALU.add)
                last.then_inc(x_up, 1)

            def t_low(p):
                dve.wait_ge(t_hi, p.nth(1, 1))
                rest(tT[1], xi, tT[0]).then_inc(t_lo, 1)

            def kp_low(p):
                dve.wait_ge(kp_hi, p.nth(1, 1))
                low = slice(DS, 2 * DS)
                V.scalar_tensor_tensor(kp[low], b_ps[low, 0:J * C].rearrange("p (j q) -> p j q", j=J), -LR,
                                       kp[low].bitcast(F32), ALU.mult, ALU.subtract).then_inc(kp_lo, 1)

            def u_low(p, j):
                dve.wait_ge(u_hi, p.nth(J, j + 1))
                rest(u[1], u_ps, u[0]).then_inc(u_lo, 1)

            def s_low(p, j):
                dve.wait_ge(sc_hi, p.nth(J, j + 1))
                rest(s_lo[p.par], s_ps[p.par], s_hi[p.par]).then_inc(sc_lo, 1)

            def squared(t, m):
                half = slice(m * CC // 2, (m + 1) * CC // 2)
                dve.wait_ge(relu_ev, t.nth(2, m + 1))
                V.tensor_tensor(act32[:, half], act32[:, half], act32[:, half], ALU.mult).then_inc(square, 1)

            def gated_mix(t, j):
                dve.wait_ge(kv_mm, t.nth(J, j + 1))
                dve.wait_ge(r_ev, t.nth(J, j + 1))
                if not (isinstance(t.pair, int) and t.off < 2):
                    dve.wait_ge(o_done, (t + -1).nth(J, 0))
                V.tensor_tensor(g[:, t.par, j], bank(t, f"mix{j}"), gate_r[:, j],
                                ALU.mult).then_inc(mix_ev, 1)

            def xn_rebuilt(p, j):
                dve.wait_ge(xres_ld[p.par], (p.pos() + 1) * 16)
                if not (isinstance(p.pair, int) and p.off < 1):
                    dve.wait_ge(out_st[j], p.nth(16, 0))
                V.tensor_scalar(o[:, j], x_res[:, p.par, j], st_keep[p.par][:, 0, j:j + 1],
                                st_keep[p.par][:, 1, j:j + 1], ALU.subtract, ALU.mult).then_inc(xn_again, 1)

            def y_added(p, j):
                dve.wait_ge(y_mm, p.nth(J, j + 1))
                dve.wait_ge(xn_again, p.nth(J, j + 1))
                V.tensor_tensor(o[:, j], y_ps, o[:, j], ALU.add).then_inc(y_add, 1)

            def step(t, main=True, prev=True, nxt=True):
                p, n = t + -1, t + 1
                if nxt:
                    stats(n)
                if prev:
                    doubled(p, LEVELS)
                if main:
                    kq_rows(t)
                if prev:
                    t_low(p)
                if main:
                    v_rows(t, 0)
                if prev:
                    xn_rebuilt(p, 0)
                if main:
                    gate_mix(t, 0)
                if prev:
                    kp_low(p)
                if main:
                    masked(t)
                    v_rows(t, 1)
                if nxt:
                    normalise(n)
                if main:
                    coupled(t, 1)
                if prev:
                    u_low(p, 0)
                if main:
                    gate_mix(t, 1)
                if prev:
                    s_low(p, 0)
                if main:
                    doubled(t, 1)
                if nxt:
                    carry_over(n)
                    first_column(n)
                if prev:
                    y_added(p, 0)
                if main:
                    squared(t, 0)
                    coupled(t, 2)
                    doubled(t, 2)
                if prev:
                    xn_rebuilt(p, 1)
                    u_low(p, 1)
                if main:
                    squared(t, 1)
                    coupled(t, 3)
                if prev:
                    s_low(p, 1)
                if main:
                    doubled(t, 3)
                if prev:
                    y_added(p, 1)
                if nxt:
                    xn_low(n)
                if main:
                    coupled(t, 4)
                if nxt:
                    key_mix(n, 0)
                if main:
                    doubled(t, 4)
                    coupled(t, 5)
                if nxt:
                    key_mix(n, 1)
                if main:
                    doubled(t, 5)
                    gated_mix(t, 0)
                    coupled(t, 6)
                    gated_mix(t, 1)

            first = Tile(0, 0)
            stats(first)
            normalise(first)
            first_column(first)
            xn_low(first)
            for m in range(2):
                key_mix(first, m)
            step(first, prev=False)
            for t in range(1, FIRST):
                step(Tile(0, t))
            with dve.Fori(0, PAIRS) as i:
                for b in range(2):
                    step(Tile(i, FIRST + b))
            step(Tile(0, NT - 1), nxt=False)
            step(Tile(0, NT), main=False, nxt=False)

        @block.tensor
        def _(pe):
            def mm(out_, lhsT, rhs, start, stop):
                return nc.tensor.matmul(out_, lhsT, rhs, start=start, stop=stop)

            def split_mm(out_, w, m, start, stop):
                mm(out_, w[1], m[0], start, False)
                mm(out_, w[0], m[0], False, False)
                return mm(out_, w[0], m[1], False, stop)

            def cut(pair, *at_):
                return pair[0][at_], pair[1][at_]

            ALL = slice(None)

            pe.wait_ge(beta_bc, 1)
            for n in range(2):
                pe.wait_ge(w_ld[n], w_count(n))
                for c in range(CC):
                    last = mm(f_ps[n][:, 0:WEIGHTS[n][1]], beta_b[:, c], staged(n)[:, c], c == 0, c == CC - 1)
                last.then_inc(bias_mm, 1)
            pe.wait_ge(dve_zero, 1)
            for i in range(2):
                nc.tensor.matmul(s_ps[i], s_hi[i][:, 0:P], s_hi[i], start=True, stop=False,
                                 skip_group_check=True)

            def xn_transposes(n, j):
                pe.wait_ge(xn_done, n.nth(1, 1))
                if n.off == 0:
                    pe.wait_ge(bias_add, 2)
                elif j == 0:
                    pe.wait_ge(v_ev, (n + -1).nth(J, 2))
                else:
                    pe.wait_ge(relu_ev, (n + -1).nth(2, 1))
                f = bank(n + -1, f"xt{j}")
                for c in range(CC):
                    last = nc.tensor.transpose(f[:, c * C:(c + 1) * C], xn[:, j, c * P:(c + 1) * P], ident)
                last.then_inc(xt_mm, 1)

            def kq(t):
                pe.wait_ge(xnT_lo, t.nth(1, 1))
                if not (isinstance(t.pair, int) and t.off < 1):
                    pe.wait_ge(mix_ev, (t + -1).nth(J, 1))
                else:
                    pe.wait_ge(w_lo, 2)
                    pe.wait_ge(xt_ev, t.nth(J, 2))
                f = bank(t, "kq")
                for j in range(J):
                    for c in range(CC):
                        last = split_mm(f[:, j * KQ:(j + 1) * KQ], cut(xnT, ALL, c, slice(j * C, (j + 1) * C)),
                                        cut(wkq, ALL, c), c == 0, c == CC - 1)
                last.then_inc(kq_mm, 1)

            def v_half(t, j, h):
                if h == 0:
                    if j == 1:
                        pe.wait_ge(kq_ev, t.nth(1, 1))
                    elif not (isinstance(t.pair, int) and t.off < 1):
                        pe.wait_ge(mix_ev, (t + -1).nth(J, 2))
                f = bank(t, f"v{j}")
                for c in (2 * h, 2 * h + 1):
                    last = split_mm(f, cut(xnT, ALL, c, slice(j * C, (j + 1) * C)), cut(wv, ALL, c),
                                    c == 0, c == CC - 1)
                if h:
                    last.then_inc(v_mm, 1)

            def k_half(t, m, h):
                if h == 0:
                    if m == 0:
                        pe.wait_ge(xk_lo, t.nth(2, 2))
                        if t.off == 0:
                            pe.wait_ge(w_lo, NW)
                        pe.wait_ge(v_ev, t.nth(J, 1))
                    elif t.off < NT - 1:
                        pe.wait_ge(xt_ev, (t + 1).nth(J, 1))
                    else:
                        pe.wait_ge(v_ev, t.nth(J, 2))
                f = bank(t, f"k{m}")
                d = 2 * m + h
                for c in range(CC):
                    last = split_mm(f[:, h * TT:(h + 1) * TT], cut(wfk, ALL, c, slice(d * P, (d + 1) * P)),
                                    cut(xkT, ALL, c), c == 0, c == CC - 1)
                if h:
                    last.then_inc(k_mm, 1)

            def r_half(t, j, h):
                if h == 0:
                    if j == 0:
                        pe.wait_ge(xr_lo, t.nth(2, 2))
                        if t.off < NT - 1:
                            pe.wait_ge(xt_ev, (t + 1).nth(J, 2))
                        else:
                            pe.wait_ge(relu_ev, t.nth(2, 1))
                    else:
                        pe.wait_ge(relu_ev, t.nth(2, 2))
                f = bank(t, f"r{j}")
                for c in (2 * h, 2 * h + 1):
                    last = split_mm(f, cut(xrT, ALL, c, slice(j * C, (j + 1) * C)), cut(wr, ALL, c),
                                    c == 0, c == CC - 1)
                if h:
                    last.then_inc(r_mm, 1)

            def kv_half(t, j, h):
                if h == 0:
                    pe.wait_ge(r_ev, t.nth(J, j + 1))
                    pe.wait_ge(act_lo, t.nth(2, 2))
                f = bank(t, f"mix{j}")
                for c in (2 * h, 2 * h + 1):
                    last = split_mm(f, cut(actT, ALL, c, slice(j * C, (j + 1) * C)), cut(wfv, ALL, c),
                                    c == 0, c == CC - 1)
                if h:
                    last.then_inc(kv_mm, 1)

            def kq_transposes(t, j):
                if j == 0:
                    pe.wait_ge(kn_lo, t.nth(1, 1))
                    pe.wait_ge(qn_lo, t.nth(1, 1))
                    if not (isinstance(t.pair, int) and t.off < 1):
                        pe.wait_ge(xT_ev, t.nth(LEVELS, 0))
                elif not (isinstance(t.pair, int) and t.off < 1):
                    pe.wait_ge(x_up, t.nth(LEVELS, 0))
                dst = (b_ps, a_ps)[j]
                rows = kn[t.par][:, j].bitcast(F32)
                nc.tensor.transpose(dst[:, 0:C], rows[:, 3 * DS:5 * DS], ident)
                nc.tensor.transpose(dst[:, C:2 * C], rows[:, DS:3 * DS], ident)
                nc.tensor.transpose(dst[:, 2 * C:3 * C], qn[:, j].bitcast(F32), ident).then_inc(kqT_mm, 1)

            def products(t):
                pe.wait_ge(kqT_ev, t.nth(J, 2))
                for j in range(J):
                    both = kqT[t.par][:, j, 1:3].rearrange("p k q -> p (k q)")
                    dst = a_ps[:, 2 * j * C:2 * (j + 1) * C]
                    mm(dst, kqT[t.par][:, j, 1], both, True, False)
                    last = mm(dst, kqT[t.par][:, j, 0], both, False, True)
                last.then_inc(g_mm, 1)

            def couple_blocks(t, i):
                if i == 1:
                    pe.wait_ge(mt_ev, t.nth(1, 1))
                    pe.wait_ge(x0_done, t.nth(1, 1))
                    if not (isinstance(t.pair, int) and t.off < 1):
                        pe.wait_ge(kp_lo, t.nth(1, 0))
                else:
                    pe.wait_ge(x_up, t.nth(LEVELS, i - 1))
                for j in range(J):
                    last = mm(a_ps[:, j * C // 2:(j + 1) * C // 2].rearrange("p (n b) -> p n b", b=2 ** i),
                              mt[:, j], second_halves(xi, i)[:, j], True, True)
                last.then_inc(ox_mm, 1)
                for j in range(J):
                    last = nc.tensor.transpose(b_ps[:, j * C:(j + 1) * C], xi[:, j], ident)
                last.then_inc(xT_mm, 1)

            def double_blocks(t, i):
                pe.wait_ge(ox_ev, t.nth(LEVELS, i))
                pe.wait_ge(xT_ev, t.nth(LEVELS, i))
                for j in range(J):
                    last = mm(a_ps[:, (J + j) * C // 2:(J + j + 1) * C // 2], xiT[:, j], ox[:, j], True, True)
                last.then_inc(xox_mm, 1)

            def tk(p):
                pe.wait_ge(t_lo, p.nth(1, 1))
                if p.off < NT - 1:
                    pe.wait_ge(kqT_ev, (p + 1).nth(J, 1))
                for j in range(J):
                    rows = kn[p.par][:, j]
                    last = split_mm(b_ps[:, j * C:(j + 1) * C], (rows[:, 0:2 * DS], rows[:, 2 * DS:4 * DS]),
                                    cut(tT, ALL, j), True, True)
                last.then_inc(kp_mm, 1)

            def u_and_qs(p, j):
                if j == 0:
                    pe.wait_ge(kp_lo, p.nth(1, 1))
                    pe.wait_ge(v_lo, p.nth(J, 2))
                if j or not (isinstance(p.pair, int) and p.off < 1):
                    pe.wait_ge(u_lo, p.nth(J, j))
                    pe.wait_ge(sc_lo, p.nth(J, j))
                split_mm(u_ps, cut(tT, ALL, j), cut(v[p.par], ALL, j), True, False)
                mm(u_ps, kp[:, j], s_hi[p.par], False, False)
                mm(u_ps, kp[:, j], s_lo[p.par], False, True).then_inc(u_mm, 1)
                if j or not (isinstance(p.pair, int) and p.off < 1):
                    pe.wait_ge(y_add, p.nth(J, j))
                mm(y_ps, kqT[p.par][:, j, 2], s_hi[p.par], True, False)
                mm(y_ps, kqT[p.par][:, j, 2], s_lo[p.par], False, False)

            def s_and_y(p, j):
                pe.wait_ge(u_lo, p.nth(J, j + 1))
                rows = kn[p.par][:, j]
                for w, m in ((0, 0), (1, 0), (0, 1)):
                    last = nc.tensor.matmul(s_ps[p.par], rows[:, 2 * w * DS:2 * (w + 1) * DS], u[m],
                                            start=False, stop=False, skip_group_check=True)
                last.then_inc(s_mm, 1)
                pe.wait_ge(at_lo, p.nth(1, 1))
                split_mm(y_ps, cut(at[p.par], ALL, j), u, False, True).then_inc(y_mm, 1)

            def step(t, main=True, prev=True, nxt=True):
                p, n = t + -1, t + 1
                if main:
                    kq(t)
                if prev:
                    double_blocks(p, LEVELS)
                if main:
                    v_half(t, 0, 0)
                    v_half(t, 0, 1)
                    kq_transposes(t, 0)
                    kq_transposes(t, 1)
                    v_half(t, 1, 0)
                if prev:
                    tk(p)
                if main:
                    products(t)
                    v_half(t, 1, 1)
                if prev:
                    u_and_qs(p, 0)
                if main:
                    couple_blocks(t, 1)
                    k_half(t, 0, 0)
                if prev:
                    s_and_y(p, 0)
                if main:
                    double_blocks(t, 1)
                if nxt:
                    xn_transposes(n, 0)
                if main:
                    k_half(t, 0, 1)
                    couple_blocks(t, 2)
                    k_half(t, 1, 0)
                    double_blocks(t, 2)
                if nxt:
                    xn_transposes(n, 1)
                if prev:
                    u_and_qs(p, 1)
                if main:
                    k_half(t, 1, 1)
                    couple_blocks(t, 3)
                    r_half(t, 0, 0)
                if prev:
                    s_and_y(p, 1)
                if main:
                    double_blocks(t, 3)
                    r_half(t, 0, 1)
                    couple_blocks(t, 4)
                    r_half(t, 1, 0)
                    double_blocks(t, 4)
                    r_half(t, 1, 1)
                    couple_blocks(t, 5)
                    kv_half(t, 0, 0)
                    double_blocks(t, 5)
                    kv_half(t, 0, 1)
                    couple_blocks(t, 6)
                    kv_half(t, 1, 0)
                    kv_half(t, 1, 1)

            pe.wait_ge(consts, 1)
            for j in range(J):
                xn_transposes(Tile(0, 0), j)
            step(Tile(0, 0), prev=False)
            for t in range(1, FIRST):
                step(Tile(0, t))
            with pe.Fori(0, PAIRS) as i:
                for b in range(2):
                    step(Tile(i, FIRST + b))
            step(Tile(0, NT - 1), nxt=False)
            step(Tile(0, NT), main=False, nxt=False)


def kernel(L0_attn_x, L0_attn_Wk, L0_attn_bk, L0_attn_Wv, L0_attn_bv, L0_attn_Wq, L0_attn_bq, L0_attn_gamma,
           L0_attn_beta, L0_ffn_W_r, L0_ffn_W_k, L0_ffn_W_v, L0_ffn_mu_r, L0_ffn_mu_k):
    import numpy as np
    import concourse.bacc as bacc
    from concourse.bass_utils import run_bass_kernel_spmd

    def by_channel(a):
        return np.transpose(np.reshape(a, (-1, 128)))

    arrays = {
        "x": L0_attn_x, "Wk_t": np.transpose(L0_attn_Wk), "bk": L0_attn_bk, "Wv_t": np.transpose(L0_attn_Wv),
        "bv": L0_attn_bv, "Wq_t": np.transpose(L0_attn_Wq), "bq": L0_attn_bq, "gamma": by_channel(L0_attn_gamma),
        "beta": by_channel(L0_attn_beta), "Wr_t": np.transpose(L0_ffn_W_r), "Wfk_t": np.transpose(L0_ffn_W_k),
        "Wfv_t": np.transpose(L0_ffn_W_v), "mu_r": by_channel(L0_ffn_mu_r), "mu_k": by_channel(L0_ffn_mu_k),
    }
    arrays = {name: np.ascontiguousarray(a) for name, a in arrays.items()}
    nc = bacc.Bacc("TRN2", target_bir_lowering=False, num_devices=1)
    args = [nc.dram_tensor(name, a.shape, mybir.dt.from_np(a.dtype), kind="ExternalInput").ap()
            for name, a in arrays.items()]
    out = nc.dram_tensor("out", arrays["x"].shape, F32, kind="ExternalOutput").ap()
    build(nc, *args, out)
    result = run_bass_kernel_spmd(nc, [arrays], core_ids=[0])
    return result.results[0]["out"]
```

```python
from contextlib import ExitStack

import concourse.bass as bass
from concourse import mybir

F32 = mybir.dt.float32
F32R = mybir.dt.float32r
BF16 = mybir.dt.bfloat16
ALU = mybir.AluOpType
ACT = mybir.ActivationFunctionType

LR = 0.01
EPS = 1e-5


class Tile:

    def __init__(self, pair, off):
        self.pair, self.off = pair, off
        self.par = off % 2

    def __add__(self, n):
        return Tile(self.pair, self.off + n)

    def nth(self, per, k):
        n = per * self.off + k
        return n if isinstance(self.pair, int) else self.pair * (2 * per) + n

    def pos(self):
        return self.off // 2 if isinstance(self.pair, int) else self.pair + self.off // 2


def build(nc, x, Wkq_t, bkq, Wv_t, bv, columns, Wr_t, Wfk_t, Wfv_t, out):
    P = 128
    B, S, D = x.shape
    KQ = Wkq_t.shape[1]
    DS = KQ // 2
    CC = D // P
    C = P
    J = 2
    TT = J * C
    assert B == 2 and KQ == P
    NT = B * S // TT
    LEVELS = 6
    assert 2 ** (LEVELS + 1) == C

    x_v = x.rearrange("b (n q) d -> b n q d", q=TT)
    x_chunks = x.rearrange("b (n q) d -> b n q d", q=C)
    out_v = out.rearrange("b (n q) d -> b n q d", q=C)

    def w_view(w):
        return w.rearrange("(c p) n -> p c n", p=P)

    ctx = ExitStack()
    with ctx:
        def sb(name, shape, dt=F32):
            return ctx.enter_context(nc.sbuf_tensor(name, shape, dt))[:]

        def pb(name):
            return ctx.enter_context(nc.psum_tensor(name, [P, 512], F32))[:]

        def sem(name):
            return ctx.enter_context(nc.semaphore(name))

        def halves(name, shape):
            return sb(name + "_hi", shape, F32R), sb(name + "_lo", shape, F32R)

        wkq = halves("wkq", [P, CC, KQ])
        wv = halves("wv", [P, CC, D])
        wr = halves("wr", [P, CC, D])
        wfk = halves("wfk", [P, CC, D])
        wfv = halves("wfv", [P, CC, D])
        cols = sb("cols", [P, 4, CC])
        bias_v = sb("bias_v", [P, D])
        bias_kq = sb("bias_kq", [P, KQ])
        ident = sb("ident", [P, P])
        strict = sb("strict", [P, J, C], BF16)
        upper = sb("upper", [P, C], BF16)
        pairs = sb("pairs", [P, J, C], BF16)
        couple = sb("couple", [P, LEVELS, C], BF16)
        pick = sb("pick", [P, LEVELS, 2, C], BF16)
        spare = sb("spare", [P, 1])
        small = sb("small", [P, 4, J])
        ones = sb("ones", [P, 4, J])

        x_in = sb("x_in", [P, J, D])
        bn = sb("bn", [P, J, 6])
        mv = sb("mv", [P, J, 2])
        st = sb("st", [P, 4, J])
        st_tmp = sb("st_tmp", [P, 4, J])
        st_keep = [sb(f"st_keep{i}", [P, 4, J]) for i in range(2)]
        xn = sb("xn", [P, J, D])
        xt = sb("xt", [P, CC, TT + 1])
        carry = [sb(f"carry{i}", [P, CC, 1]) for i in range(2)]
        dx = sb("dx", [P, CC, TT])
        mix = sb("mix", [P, CC // 2, TT])
        beta_b = mix.rearrange("p c q -> p (c q)").rearrange("p (c q) -> p c q", c=CC)
        kqT32 = mix[:, 0]
        xnT = halves("xnT", [P, CC, TT])
        xkT = halves("xkT", [P, CC, TT])
        xrT = halves("xrT", [P, CC, TT])

        kq32 = sb("kq32", [P, J, KQ])
        kn = [sb(f"kn{i}", [P, J, 5 * DS], F32R) for i in range(2)]
        qn = sb("qn", [P, J, 2 * DS], F32R)
        kqT = sb("kqT", [P, J, 4, C], F32R)
        KQT_OUT = (slice(0, 3), slice(1, 4))
        KQT_Q = (0, 3)
        KQT_KQ = (slice(0, 2), slice(1, 4, 2))
        IS_K = (1, 0)
        v32 = sb("v32", [P, D])
        v = [halves(f"v{i}", [P, J, D]) for i in range(2)]
        at32 = kq32
        at = [halves(f"at{i}", [P, J, C]) for i in range(2)]
        z = sb("z", [P, C])
        y = sb("y", [P, C])
        ypick = sb("ypick", [P, J, C])
        lastT = sb("lastT", [P, C])
        ox = sb("ox", [P, C])
        tT = halves("tT", [P, J, C])
        kp = sb("kp", [P, J, C], F32R)
        act32 = sb("act32", [P, CC, TT])
        actT = halves("actT", [P, CC, TT])
        gate_r = sb("gate_r", [P, J, D])
        g = sb("g", [P, 2, J, D])

        s_hi = [sb(f"s_hi{i}", [P, D], F32R) for i in range(2)]
        s_lo = [sb(f"s_lo{i}", [P, D], F32R) for i in range(2)]
        u = halves("u", [P, D])
        x_res = sb("x_res", [P, 2, J, D])
        o = sb("o", [P, J, D])

        s_ps = [pb(f"s_ps{i}") for i in range(2)]
        u_ps = pb("u_ps")
        y_ps = pb("y_ps")
        f_ps = [pb(f"f_ps{i}") for i in range(2)]
        a_ps = pb("a_ps")
        b_ps = pb("b_ps")

        cols_ld = sem("cols_ld")
        bias_ld = sem("bias_ld")
        w_ld = [sem(f"w_ld{i}") for i in range(5)]
        x_ld = sem("x_ld")
        xres_ld = [sem(f"xres_ld{i}") for i in range(2)]
        out_st = [sem(f"out_st{i}") for i in range(J)]
        small_done = sem("small_done")
        pick_first = sem("pick_first")
        pick_sum = sem("pick_sum")
        masks_filled = sem("masks_filled")
        ident_done = sem("ident_done")
        couple0 = sem("couple0")
        consts = sem("consts")
        dve_zero = sem("dve_zero")
        beta_bc = sem("beta_bc")
        bias_mm = sem("bias_mm")
        bias_add = sem("bias_add")
        w_hi = sem("w_hi")
        w_lo_dve = sem("w_lo_dve")
        w_lo_pool = sem("w_lo_pool")
        bn_done = sem("bn_done")
        mv_done = sem("mv_done")
        st_step = sem("st_step")
        st_done = sem("st_done")
        kept = sem("kept")
        xn_done = sem("xn_done")
        xt_mm = sem("xt_mm")
        carried = sem("carried")
        xt_first = sem("xt_first")
        xt_ev = sem("xt_ev")
        xnT_hi = sem("xnT_hi")
        xnT_lo = sem("xnT_lo")
        dx_done = sem("dx_done")
        xk_mix = sem("xk_mix")
        xk_hi = sem("xk_hi")
        xk_lo = sem("xk_lo")
        xr_mix = sem("xr_mix")
        xr_hi = sem("xr_hi")
        xr_lo = sem("xr_lo")
        kq_mm = sem("kq_mm")
        kq_copied = sem("kq_copied")
        kq_back = sem("kq_back")
        kq_ev = sem("kq_ev")
        kn_hi = sem("kn_hi")
        kn_lo = sem("kn_lo")
        qn_hi = sem("qn_hi")
        qn_lo = sem("qn_lo")
        kqT_mm = sem("kqT_mm")
        kqT_ev = sem("kqT_ev")
        g_mm = sem("g_mm")
        z_parts = sem("z_parts")
        pair_parts = sem("pair_parts")
        z_done = sem("z_done")
        y_pairs = sem("y_pairs")
        y0_done = sem("y0_done")
        picked = sem("picked")
        yT_mm = sem("yT_mm")
        t_done = sem("t_done")
        at_ev = sem("at_ev")
        at_hi = sem("at_hi")
        at_lo = sem("at_lo")
        xT_mm = sem("xT_mm")
        ox_mm = sem("ox_mm")
        xox_mm = sem("xox_mm")
        ox_ev = sem("ox_ev")
        xT_ev = sem("xT_ev")
        x_up = sem("x_up")
        t_hi = sem("t_hi")
        t_lo = sem("t_lo")
        kp_mm = sem("kp_mm")
        kp_hi = sem("kp_hi")
        kp_lo = sem("kp_lo")
        v_mm = sem("v_mm")
        v_ev = sem("v_ev")
        v_hi = sem("v_hi")
        v_lo = sem("v_lo")
        k_mm = sem("k_mm")
        relu_ev = sem("relu_ev")
        square = sem("square")
        act_hi = sem("act_hi")
        act_lo = sem("act_lo")
        r_mm = sem("r_mm")
        r_ev = sem("r_ev")
        kv_mm = sem("kv_mm")
        mix_ev = sem("mix_ev")
        sig = sem("sig")
        g_done = sem("g_done")
        u_mm = sem("u_mm")
        u_hi = sem("u_hi")
        u_lo = sem("u_lo")
        s_mm = sem("s_mm")
        sc_hi = sem("sc_hi")
        sc_lo = sem("sc_lo")
        y_mm = sem("y_mm")
        xn_again = sem("xn_again")
        y_add = sem("y_add")
        gated = sem("gated")
        o_done = sem("o_done")

        HC = CC // 2
        WEIGHTS = [(wkq, (kq32, ypick)), (wv, (dx.rearrange("p c q -> p (c q)").rearrange(
                       "p (c n) -> p c n", n=D), g[:, 1])), (wfk, (act32.rearrange("p c q -> p (c q)").rearrange(
                       "p (c n) -> p c n", n=D), x_res[:, 0])),
                   (wr, (gate_r, g[:, 0])), (wfv, (o, x_res[:, 1]))]
        NW = len(WEIGHTS)
        SCALED = 2

        FIRST = 3
        PAIRS = (NT - 1 - FIRST) // 2

        SECOND = {"v0", "k0", "xt1", "r0", "mix0"}

        def bank(t, what):
            return f_ps[(t.par + (what in SECOND)) % 2]

        block = ctx.enter_context(nc.Block())

        @block.sync
        def _(sp):
            def load_x(n):
                src = x_chunks[n.par, bass.ds(n.pos() * J, J), :, :].rearrange("j q d -> q j d")
                if not (isinstance(n.pair, int) and n.off < 1):
                    sp.wait_ge(xn_done, n.nth(1, 0))
                sp.dma_start(x_in, src).then_inc(x_ld, 16)

            def load_x_res(t):
                src = x_v[t.par, bass.ds(t.pos(), 1), :, :].rearrange("a (j q) d -> q (a j) d", q=C)
                if isinstance(t.pair, int) and t.off < 2:
                    sp.wait_ge(w_lo_pool, (1, 3)[t.off])
                else:
                    sp.wait_ge(o_done, (t + -1).nth(J, 0))
                sp.dma_start(x_res[:, t.par], src).then_inc(xres_ld[t.par], 16)

            def store(p, j):
                dst = out_v[p.par, bass.ds(p.pos() * J + j, 1), :, :].rearrange("a q d -> q (a d)")
                sp.wait_ge(o_done, p.nth(J, j + 1))
                sp.dma_start(dst, o[:, j]).then_inc(out_st[j], 16)

            def step(t, main=True, prev=True, ahead=True):
                if ahead:
                    load_x(t + 2)
                if main:
                    load_x_res(t)
                if prev:
                    for j in range(J):
                        store(t + -1, j)

            load_x(Tile(0, 0))
            for n, w in enumerate((Wkq_t, Wv_t, Wfk_t, Wr_t, Wfv_t)):
                if n == 3:
                    load_x(Tile(0, 1))
                for h in range(2):
                    sp.dma_start(WEIGHTS[n][1][h], w_view(w)[:, h * HC:(h + 1) * HC]).then_inc(w_ld[n], 16)
            step(Tile(0, 0), prev=False)
            for t in range(1, FIRST):
                step(Tile(0, t))
            with sp.Fori(0, PAIRS - 1) as i:
                for b in range(2):
                    step(Tile(i, FIRST + b))
            for t in range(FIRST + 2 * (PAIRS - 1), NT + 1):
                step(Tile(0, t), main=t < NT, ahead=t + 2 < NT)
            for j in range(J):
                sp.wait_ge(out_st[j], 16 * NT)

        @block.gpsimd
        def _(pool):
            for k, value in enumerate((EPS, LR, -0.5, 1.0)):
                nc.gpsimd.memset(small[:, k], value)
            nc.gpsimd.memset(ones, 1.0).then_inc(small_done, 1)
            nc.gpsimd.memset(ident, 0.0)
            nc.gpsimd.memset(upper, 1.0)
            nc.gpsimd.memset(strict, 1.0)
            nc.gpsimd.memset(pairs, 0.0)
            nc.gpsimd.memset(pick, 1.0)
            nc.gpsimd.memset(couple, 1.0).then_inc(masks_filled, 1)

            def norm_scalars(n):
                steps = 7
                mean, var = mv[:, :, 0], mv[:, :, 1]
                eps, lr, power, one = (small[:, k] for k in range(4))
                pool.wait_ge(mv_done, n.nth(1, 1))
                if not (isinstance(n.pair, int) and n.off < 1):
                    pool.wait_ge(kept, n.nth(1, 0))
                    pool.wait_ge(xn_done, n.nth(1, 0))
                nc.gpsimd.tensor_tensor(st[:, 0], mean, one, ALU.mult).then_inc(st_step, 1)
                nc.gpsimd.tensor_tensor(st_tmp[:, 0], var, eps, ALU.add).then_inc(st_step, 1)
                pool.wait_ge(st_step, n.nth(steps, 2))
                nc.gpsimd.tensor_tensor(st[:, 1], st_tmp[:, 0], power, ALU.pow).then_inc(st_step, 1)
                pool.wait_ge(st_step, n.nth(steps, 3))
                nc.gpsimd.tensor_tensor(st_tmp[:, 1], st[:, 1], st[:, 1], ALU.mult).then_inc(st_step, 1)
                pool.wait_ge(st_step, n.nth(steps, 4))
                nc.gpsimd.tensor_tensor(st_tmp[:, 2], st_tmp[:, 1], var, ALU.mult).then_inc(st_step, 1)
                pool.wait_ge(st_step, n.nth(steps, 5))
                nc.gpsimd.tensor_tensor(st_tmp[:, 3], st_tmp[:, 2], eps, ALU.add).then_inc(st_step, 1)
                pool.wait_ge(st_step, n.nth(steps, 6))
                nc.gpsimd.tensor_tensor(st[:, 2], st_tmp[:, 3], power, ALU.pow).then_inc(st_step, 1)
                pool.wait_ge(st_step, n.nth(steps, 7))
                nc.gpsimd.tensor_tensor(st[:, 3], st[:, 2], lr, ALU.mult).then_inc(st_done, 1)

            def shift_difference(n):
                pool.wait_ge(xt_ev, n.nth(J, 2))
                pool.wait_ge(xt_first, n.nth(1, 1))
                if not (isinstance(n.pair, int) and n.off < 1):
                    pool.wait_ge(xr_mix, n.nth(2, 0))
                else:
                    pool.wait_ge(w_lo_dve, 2)
                    pool.wait_ge(bias_mm, 2)
                nc.gpsimd.tensor_tensor(dx, xt[:, :, 1:TT + 1], xt[:, :, 0:TT], ALU.subtract).then_inc(dx_done, 1)

            def xn_low(n):
                pool.wait_ge(xnT_hi, n.nth(1, 1))
                nc.gpsimd.tensor_tensor(xnT[1], xt[:, :, 1:TT + 1], xnT[0].bitcast(F32),
                                        ALU.subtract).then_inc(xnT_lo, 1)

            def keep_scalars(t):
                if not (isinstance(t.pair, int) and t.off < 2):
                    pool.wait_ge(xn_again, (t + -1).nth(J, 0))
                pool.wait_ge(st_done, t.nth(1, 1))
                nc.gpsimd.tensor_tensor(st_keep[t.par], st, ones, ALU.mult).then_inc(kept, 1)

            def v_low(t, j):
                pool.wait_ge(v_hi, t.nth(J, j + 1))
                nc.gpsimd.tensor_tensor(v[t.par][1][:, j], v32, v[t.par][0][:, j].bitcast(F32),
                                        ALU.subtract).then_inc(v_lo, 1)

            def at_low(t):
                pool.wait_ge(at_hi, t.nth(1, 1))
                nc.gpsimd.tensor_tensor(at[t.par][1], at32, at[t.par][0].bitcast(F32),
                                        ALU.subtract).then_inc(at_lo, 1)

            def act_low(t, m):
                half = slice(m * CC // 2, (m + 1) * CC // 2)
                pool.wait_ge(act_hi, t.nth(2, m + 1))
                if not (isinstance(t.pair, int) and t.off < 1):
                    pool.wait_ge(kv_mm, t.nth(J, 0))
                nc.gpsimd.tensor_tensor(actT[1][:, half], act32[:, half], actT[0][:, half].bitcast(F32),
                                        ALU.subtract).then_inc(act_lo, 1)

            def silu(t, j):
                pool.wait_ge(sig, t.nth(J, j + 1))
                nc.gpsimd.tensor_tensor(g[:, t.par, j], g[:, t.par, j], gate_r[:, j], ALU.mult).then_inc(g_done, 1)

            def output(p, j):
                pool.wait_ge(y_add, p.nth(J, j + 1))
                pool.wait_ge(g_done, p.nth(J, j + 1))
                nc.gpsimd.tensor_tensor(o[:, j], o[:, j], g[:, p.par, j], ALU.mult).then_inc(gated, 1)
                pool.wait_ge(gated, p.nth(J, j + 1))
                nc.gpsimd.tensor_tensor(o[:, j], o[:, j], x_res[:, p.par, j], ALU.add).then_inc(o_done, 1)

            def weight_low(n):
                for h in range(2):
                    hi, lo = (half[:, h * HC:(h + 1) * HC] for half in WEIGHTS[n][0])
                    pool.wait_ge(w_hi, n + 1)
                    last = nc.gpsimd.tensor_tensor(lo, WEIGHTS[n][1][h], hi.bitcast(F32), ALU.subtract)
                last.then_inc(w_lo_pool, 1)

            def step(t, main=True, prev=True, nxt=True):
                p, n = t + -1, t + 1
                first = main and t.off == 0
                if nxt and not first:
                    norm_scalars(n)
                if main:
                    v_low(t, 0)
                if first:
                    weight_low(2)
                    weight_low(3)
                if main:
                    v_low(t, 1)
                    at_low(t)
                if first:
                    weight_low(4)
                if prev:
                    output(p, 0)
                if main:
                    act_low(t, 0)
                if nxt:
                    shift_difference(n)
                if main:
                    act_low(t, 1)
                if nxt:
                    xn_low(n)
                if prev:
                    output(p, 1)
                if nxt:
                    keep_scalars(n)
                if main:
                    silu(t, 0)
                    silu(t, 1)

            pool.wait_ge(small_done, 1)
            pool.wait_ge(masks_filled, 1)
            nc.gpsimd.affine_select(out=ident, in_=ident, compare_op=ALU.not_equal, fill=1.0, base=0,
                                    pattern=[[-1, P]], channel_multiplier=1).then_inc(ident_done, 1)

            def keep(m, condition, base, columns, rows):
                return nc.gpsimd.affine_select(out=m, in_=m, compare_op=condition, fill=0.0, base=base,
                                               pattern=columns, channel_multiplier=rows)

            def halves_of(m, i):
                m = m.rearrange("p (n h b) -> p n h b", h=2, b=2 ** i)
                return m[:, :, 0], m[:, :, 1]

            keep(upper, ALU.is_ge, 0, [[1, C]], -1)
            keep(strict[:, 0], ALU.is_gt, 0, [[-1, C]], 1)
            keep(strict[:, 1], ALU.is_gt, 0, [[1, C]], -1)
            for j in range(J):
                m = pairs[:, j].rearrange("p (n h) -> p n h", h=2)[:, :, 1 - j]
                nc.gpsimd.affine_select(out=m, in_=m, compare_op=ALU.not_equal, fill=1.0, base=-j,
                                        pattern=[[-2, C // 2]], channel_multiplier=1)
            norm_scalars(Tile(0, 0))
            for i in range(1, LEVELS + 1):
                b = 2 ** i
                n = C // (2 * b)
                first_half, second_half = halves_of(pick[:, i - 1, 0], i)
                keep(first_half, ALU.is_ge, 0, [[-2 * b, n], [-1, b]], 1)
                last = keep(second_half, ALU.is_ge, b, [[2 * b, n], [1, b]], -1)
            last.then_inc(pick_first, 1)
            keep_scalars(Tile(0, 0))
            norm_scalars(Tile(0, 1))
            for i in range(1, LEVELS + 1):
                b = 2 ** i
                for h, m in enumerate(halves_of(couple[:, i - 1], i)):
                    other = (1 - h) * b
                    keep(m, ALU.is_ge, -other, [[-2 * b, C // (2 * b)], [0, b]], 1).then_inc(couple0, 1)
            shift_difference(Tile(0, 0))
            for i in range(1, LEVELS + 1):
                b = 2 ** i
                for h, m in enumerate(halves_of(couple[:, i - 1], i)):
                    pool.wait_ge(couple0, 2 * i)
                    last = keep(m, ALU.is_ge, (1 - h) * b + b - 1, [[2 * b, C // (2 * b)], [0, b]], -1)
            last.then_inc(consts, 1)
            step(Tile(0, 0), prev=False)
            for t in range(1, FIRST):
                step(Tile(0, t))
            with pool.Fori(0, PAIRS) as i:
                for b in range(2):
                    step(Tile(i, FIRST + b))
            step(Tile(0, NT - 1), nxt=False)
            step(Tile(0, NT), main=False, nxt=False)

        @block.scalar
        def _(act):
            act.dma_start(cols, columns).then_inc(cols_ld, 16)
            act.dma_start(bias_kq, bkq.partition_broadcast(P)).then_inc(bias_ld, 16)
            act.dma_start(bias_v, bv.partition_broadcast(P)).then_inc(bias_ld, 16)

            def copy(out_, in_, **kw):
                return nc.scalar.activation(out_, in_, ACT.Copy, **kw)

            def weight_high(n):
                act.wait_ge(w_ld[n], 32)
                if n == 0:
                    act.wait_ge(cols_ld, 16)
                for c in range(CC):
                    last = copy(WEIGHTS[n][0][0][:, c], WEIGHTS[n][1][c // HC][:, c % HC],
                                **({"scale": cols[:, 0, c:c + 1]} if n < SCALED else {}))
                last.then_inc(w_hi, 1)

            def transposed(n, j):
                act.wait_ge(xt_mm, n.nth(J, j + 1))
                if j == 0 and not (isinstance(n.pair, int) and n.off < 1):
                    act.wait_ge(carried, n.nth(1, 0))
                    act.wait_ge(xr_mix, n.nth(2, 0))
                    act.wait_ge(xnT_lo, n.nth(1, 0))
                f = bank(n + -1, f"xt{j}")
                copy(xt[:, :, 1 + j * C:1 + (j + 1) * C],
                     f.rearrange("p (c q) -> p c q", c=CC)).then_inc(xt_ev, 1)

            def xn_high(n):
                act.wait_ge(xt_ev, n.nth(J, 2))
                if not (isinstance(n.pair, int) and n.off < 1):
                    act.wait_ge(v_mm, n.nth(J, 0))
                copy(xnT[0], xt[:, :, 1:TT + 1]).then_inc(xnT_hi, 1)

            def kq_copy(t):
                act.wait_ge(kq_mm, t.nth(1, 1))
                if not (isinstance(t.pair, int) and t.off < 1):
                    act.wait_ge(xr_lo, t.nth(2, 1))
                copy(kqT32, bank(t, "kq")[:, 0:TT]).then_inc(kq_copied, 1)

            def kqT_copy(t, j):
                act.wait_ge(kqT_mm, t.nth(J, j + 1))
                src = (b_ps, a_ps)[j]
                copy(kqT[:, j, KQT_OUT[t.par]], src[:, 0:3 * C].rearrange("p (k q) -> p k q", k=3)).then_inc(kqT_ev, 1)

            def v_high(t, j):
                act.wait_ge(v_ev, t.nth(J, j + 1))
                copy(v[t.par][0][:, j], v32).then_inc(v_hi, 1)

            def at_high(t):
                act.wait_ge(at_ev, t.nth(1, 1))
                copy(at[t.par][0], at32).then_inc(at_hi, 1)

            def x_transposed(t, i):
                act.wait_ge(xT_mm, t.nth(LEVELS, i))
                copy(lastT, b_ps[:, 0:C]).then_inc(xT_ev, 1)

            def t_high(p):
                act.wait_ge(t_done, p.nth(1, 1))
                if not (isinstance(p.pair, int) and p.off < 1):
                    act.wait_ge(u_mm, p.nth(J, 0))
                copy(tT[0], ypick).then_inc(t_hi, 1)

            def kp_high(p):
                act.wait_ge(kp_mm, p.nth(1, 1))
                copy(kp, b_ps[:, 0:J * C].rearrange("p (j q) -> p j q", j=J), scale=-LR).then_inc(kp_hi, 1)

            def u_high(p, j):
                act.wait_ge(u_mm, p.nth(J, j + 1))
                if j or not (isinstance(p.pair, int) and p.off < 1):
                    act.wait_ge(y_mm, p.nth(J, j))
                copy(u[0], u_ps).then_inc(u_hi, 1)

            def s_high(p, j):
                act.wait_ge(s_mm, p.nth(J, j + 1))
                copy(s_hi[p.par], s_ps[p.par]).then_inc(sc_hi, 1)

            def relu(t, m):
                act.wait_ge(k_mm, t.nth(2, m + 1))
                if not (isinstance(t.pair, int) and t.off < 1):
                    act.wait_ge(act_lo, t.nth(2, 0))
                hidden = bank(t, f"k{m}").rearrange("p (c q) -> p c q", c=2)
                nc.scalar.activation(act32[:, 2 * m:2 * m + 2], hidden, ACT.Relu).then_inc(relu_ev, 1)

            def act_high(t, m):
                act.wait_ge(square, t.nth(2, m + 1))
                if not (isinstance(t.pair, int) and t.off < 1):
                    act.wait_ge(kv_mm, t.nth(J, 0))
                copy(actT[0][:, 2 * m:2 * m + 2], act32[:, 2 * m:2 * m + 2]).then_inc(act_hi, 1)

            def sigmoid_r(t, j):
                act.wait_ge(r_mm, t.nth(J, j + 1))
                if not (isinstance(t.pair, int) and t.off < 1):
                    act.wait_ge(g_done, t.nth(J, 0))
                nc.scalar.activation(gate_r[:, j], bank(t, f"r{j}"), ACT.Sigmoid).then_inc(r_ev, 1)

            def sigmoid_mix(t, j):
                act.wait_ge(mix_ev, t.nth(J, j + 1))
                nc.scalar.activation(gate_r[:, j], g[:, t.par, j], ACT.Sigmoid).then_inc(sig, 1)

            def step(t, main=True, prev=True, nxt=True):
                p, n = t + -1, t + 1
                first = main and t.off == 0
                if main and not first:
                    kq_copy(t)
                if prev:
                    t_high(p)
                if main:
                    kqT_copy(t, 0)
                    kqT_copy(t, 1)
                    v_high(t, 0)
                if prev:
                    kp_high(p)
                    u_high(p, 0)
                if main:
                    at_high(t)
                    v_high(t, 1)
                    x_transposed(t, 1)
                if nxt:
                    transposed(n, 0)
                if prev:
                    s_high(p, 0)
                if main:
                    relu(t, 0)
                    x_transposed(t, 2)
                    act_high(t, 0)
                if nxt:
                    transposed(n, 1)
                if prev:
                    u_high(p, 1)
                if main:
                    relu(t, 1)
                    x_transposed(t, 3)
                if prev:
                    s_high(p, 1)
                if nxt:
                    xn_high(n)
                if main:
                    act_high(t, 1)
                    x_transposed(t, 4)
                    sigmoid_r(t, 0)
                    x_transposed(t, 5)
                    sigmoid_r(t, 1)
                    x_transposed(t, 6)
                    sigmoid_mix(t, 0)
                    sigmoid_mix(t, 1)

            weight_high(0)
            for j in range(J):
                transposed(Tile(0, 0), j)
            xn_high(Tile(0, 0))
            weight_high(1)
            weight_high(2)
            kq_copy(Tile(0, 0))
            weight_high(3)
            weight_high(4)
            step(Tile(0, 0), prev=False)
            for t in range(1, FIRST):
                step(Tile(0, t))
            with act.Fori(0, PAIRS) as i:
                for b in range(2):
                    step(Tile(i, FIRST + b))
            step(Tile(0, NT - 1), nxt=False)
            step(Tile(0, NT), main=False, nxt=False)

        @block.vector
        def _(dve):
            V = nc.vector

            def rounded(out_, in_):
                return V.tensor_copy(out_, in_)

            def rest(out_, in_, hi):
                return V.tensor_tensor(out_, in_, hi.bitcast(F32), ALU.subtract)

            for i in range(2):
                V.memset(s_hi[i].bitcast(F32), 0.0)
                V.memset(s_lo[i].bitcast(F32), 0.0)
                V.memset(carry[i], 0.0)
            V.memset(xt[:, :, 0:1], 0.0).then_inc(dve_zero, 1)

            def weight_low(n):
                dve.wait_ge(w_hi, n + 1)
                for c in range(CC):
                    last = V.scalar_tensor_tensor(WEIGHTS[n][0][1][:, c], WEIGHTS[n][1][c // HC][:, c % HC],
                                                  cols[:, 0, c:c + 1], WEIGHTS[n][0][0][:, c].bitcast(F32),
                                                  ALU.mult, ALU.subtract)
                last.then_inc(w_lo_dve, 1)

            def stats(n):
                dve.wait_ge(x_ld, n.nth(16, 16))
                for j in range(J):
                    last = V.bn_stats(bn[:, j], x_in[:, j])
                last.then_inc(bn_done, 1)
                if not (isinstance(n.pair, int) and n.off < 1):
                    dve.wait_ge(st_done, n.nth(1, 0))
                dve.wait_ge(bn_done, n.nth(1, 1))
                V.memset(spare, 0.0)
                for j in range(J):
                    last = V.bn_aggr(mv[:, j], bn[:, j])
                last.then_inc(mv_done, 1)

            def normalise(n):
                dve.wait_ge(st_done, n.nth(1, 1))
                if not (isinstance(n.pair, int) and n.off < 1):
                    dve.wait_ge(xt_mm, n.nth(J, 0))
                for j in range(J):
                    last = V.tensor_scalar(xn[:, j], x_in[:, j], st[:, 0, j:j + 1], st[:, 1, j:j + 1],
                                           ALU.subtract, ALU.mult)
                last.then_inc(xn_done, 1)

            def carry_over(n):
                before = n + -1
                dve.wait_ge(xt_ev, before.nth(J, 2))
                V.tensor_copy(carry[before.par], xt[:, :, TT:TT + 1]).then_inc(carried, 1)

            def first_column(n):
                if not (isinstance(n.pair, int) and n.off < 1):
                    dve.wait_ge(carried, n.nth(1, 0))
                    dve.wait_ge(dx_done, n.nth(1, 0))
                    dve.wait_ge(xr_mix, n.nth(2, 0))
                V.tensor_copy(xt[:, :, 0:1], carry[n.par]).then_inc(xt_first, 1)

            def xn_low(n):
                dve.wait_ge(xnT_hi, n.nth(1, 1))
                rest(xnT[1], xt[:, :, 1:TT + 1], xnT[0]).then_inc(xnT_lo, 1)

            def mixed(n, m, mu, made):
                for i in range(HC):
                    c = m * HC + i
                    last = V.scalar_tensor_tensor(mix[:, i], dx[:, c], cols[:, mu, c:c + 1], xt[:, c, 0:TT],
                                                  ALU.mult, ALU.add)
                last.then_inc(made, 1)

            def mixed_halves(n, m, dst, made, hi, lo):
                part = slice(m * HC, (m + 1) * HC)
                dve.wait_ge(made, n.nth(2, m + 1))
                rounded(dst[0][:, part], mix).then_inc(hi, 1)
                dve.wait_ge(hi, n.nth(2, m + 1))
                rest(dst[1][:, part], mix, dst[0][:, part]).then_inc(lo, 1)

            def key_mix(n, m):
                if m:
                    dve.wait_ge(xk_lo, n.nth(2, 1))
                else:
                    dve.wait_ge(dx_done, n.nth(1, 1))
                    dve.wait_ge(xt_first, n.nth(1, 1))
                mixed(n, m, 3, xk_mix)

            def key_halves(n, m):
                if m == 0 and not (isinstance(n.pair, int) and n.off < 1):
                    dve.wait_ge(k_mm, n.nth(2, 0))
                mixed_halves(n, m, xkT, xk_mix, xk_hi, xk_lo)

            def gate_mix(n, m):
                if m:
                    dve.wait_ge(xr_lo, n.nth(2, 1))
                else:
                    dve.wait_ge(xk_lo, n.nth(2, 2))
                mixed(n, m, 2, xr_mix)
                if m == 0 and not (isinstance(n.pair, int) and n.off < 1):
                    dve.wait_ge(r_mm, n.nth(J, 0))
                mixed_halves(n, m, xrT, xr_mix, xr_hi, xr_lo)

            def kq_rows(t):
                dve.wait_ge(kq_back, t.nth(1, 1))
                dve.wait_ge(kept, t.nth(1, 1))
                if not (isinstance(t.pair, int) and t.off < 1):
                    dve.wait_ge(at_lo, t.nth(1, 0))
                f = bank(t, "kq")
                for j in range(J):
                    rows_j = f[:, TT + j * C:TT + (j + 1) * C]
                    last = V.scalar_tensor_tensor(kq32[:, j], rows_j, st_keep[t.par][:, 2, j:j + 1], bias_kq,
                                                  ALU.mult, ALU.add)
                last.then_inc(kq_ev, 1)
                dve.wait_ge(kq_ev, t.nth(1, 1))
                rows = kn[t.par].rearrange("p j (b e) -> p j b e", e=DS)
                for j in range(J):
                    k32 = kq32[:, j, 0:DS].unsqueeze(1).to_broadcast([P, 2, DS])
                    last = rounded(rows[:, j, 0:2], k32)
                rounded(rows[:, :, 4], kq32[:, :, 0:DS]).then_inc(kn_hi, 1)
                rounded(qn[:, :, 0:DS], kq32[:, :, DS:KQ]).then_inc(qn_hi, 1)
                dve.wait_ge(kn_hi, t.nth(1, 1))
                for j in range(J):
                    k32 = kq32[:, j, 0:DS].unsqueeze(1).to_broadcast([P, 2, DS])
                    last = rest(rows[:, j, 2:4], k32, rows[:, j, 0:2])
                last.then_inc(kn_lo, 1)
                dve.wait_ge(qn_hi, t.nth(1, 1))
                rest(qn[:, :, DS:KQ], kq32[:, :, DS:KQ], qn[:, :, 0:DS]).then_inc(qn_lo, 1)

            def v_rows(t, j):
                dve.wait_ge(v_mm, t.nth(J, j + 1))
                if j or not (isinstance(t.pair, int) and t.off < 1):
                    dve.wait_ge(v_lo, t.nth(J, j))
                V.scalar_tensor_tensor(v32, bank(t, f"v{j}"), st_keep[t.par][:, 3, j:j + 1],
                                       bias_v, ALU.mult, ALU.add).then_inc(v_ev, 1)

            def masked(t):
                dve.wait_ge(g_mm, t.nth(1, 1))
                if t.off == 0:
                    dve.wait_ge(consts, 1)
                    dve.wait_ge(ident_done, 1)
                src = a_ps.rearrange("p (j k q) -> p j k q", j=J, k=2)
                keys, queries = src[:, :, IS_K[t.par]], src[:, :, 1 - IS_K[t.par]]
                if not (isinstance(t.pair, int) and t.off < 1):
                    dve.wait_ge(t_lo, t.nth(1, 0))
                V.scalar_tensor_tensor(ypick, keys, -LR, strict, ALU.mult, ALU.mult).then_inc(z_parts, 1)
                V.scalar_tensor_tensor(y, keys[:, 0], -LR, pairs[:, 0], ALU.mult, ALU.mult)
                V.scalar_tensor_tensor(lastT, keys[:, 1], -LR, pairs[:, 1], ALU.mult, ALU.mult).then_inc(pair_parts, 1)
                dve.wait_ge(z_parts, t.nth(1, 1))
                V.tensor_tensor(z, ypick[:, 0], ypick[:, 1], ALU.add).then_inc(z_done, 1)
                dve.wait_ge(pair_parts, t.nth(1, 1))
                V.tensor_tensor(y, y, lastT, ALU.add).then_inc(y_pairs, 1)
                V.tensor_tensor(at32, queries, strict[:, 1].unsqueeze(1).to_broadcast([P, J, C]),
                                ALU.mult).then_inc(at_ev, 1)
                dve.wait_ge(y_pairs, t.nth(1, 1))
                V.tensor_tensor(y, y, ident, ALU.add).then_inc(y0_done, 1)
                dve.wait_ge(y0_done, t.nth(1, 1))
                pick_factors(t, 1)

            def pick_factors(t, i):
                if i > 1:
                    dve.wait_ge(x_up, t.nth(LEVELS, i - 1))
                V.tensor_tensor(ypick, y.unsqueeze(1).to_broadcast([P, 2, C]), pick[:, i - 1],
                                ALU.mult).then_inc(picked, 1)

            def coupled(t, i):
                dve.wait_ge(ox_mm, t.nth(LEVELS, i))
                V.tensor_tensor(ox, a_ps[:, 0:C], couple[:, i - 1], ALU.mult).then_inc(ox_ev, 1)

            def doubled(t, i):
                dve.wait_ge(xox_mm, t.nth(LEVELS, i))
                V.tensor_tensor(y, a_ps[:, C:2 * C], y, ALU.add).then_inc(x_up, 1)
                if i < LEVELS:
                    pick_factors(t, i + 1)

            def inverse_done(p):
                dve.wait_ge(x_up, p.nth(LEVELS, LEVELS))
                V.tensor_tensor(ypick[:, 0], y, upper, ALU.mult)
                dve.wait_ge(yT_mm, p.nth(1, 1))
                V.tensor_tensor(ypick[:, 1], b_ps[:, 0:C], upper, ALU.mult).then_inc(t_done, 1)

            def t_low(p):
                dve.wait_ge(t_hi, p.nth(1, 1))
                rest(tT[1], ypick, tT[0]).then_inc(t_lo, 1)

            def kp_low(p):
                dve.wait_ge(kp_hi, p.nth(1, 1))
                low = slice(DS, 2 * DS)
                V.scalar_tensor_tensor(kp[low], b_ps[low, 0:J * C].rearrange("p (j q) -> p j q", j=J), -LR,
                                       kp[low].bitcast(F32), ALU.mult, ALU.subtract).then_inc(kp_lo, 1)

            def u_low(p, j):
                dve.wait_ge(u_hi, p.nth(J, j + 1))
                rest(u[1], u_ps, u[0]).then_inc(u_lo, 1)

            def s_low(p, j):
                dve.wait_ge(sc_hi, p.nth(J, j + 1))
                rest(s_lo[p.par], s_ps[p.par], s_hi[p.par]).then_inc(sc_lo, 1)

            def squared(t, m):
                half = slice(m * CC // 2, (m + 1) * CC // 2)
                dve.wait_ge(relu_ev, t.nth(2, m + 1))
                V.tensor_tensor(act32[:, half], act32[:, half], act32[:, half], ALU.mult).then_inc(square, 1)

            def gated_mix(t, j):
                dve.wait_ge(kv_mm, t.nth(J, j + 1))
                dve.wait_ge(r_ev, t.nth(J, j + 1))
                if not (isinstance(t.pair, int) and t.off < 2):
                    dve.wait_ge(o_done, (t + -1).nth(J, 0))
                V.tensor_tensor(g[:, t.par, j], bank(t, f"mix{j}"), gate_r[:, j],
                                ALU.mult).then_inc(mix_ev, 1)

            def xn_rebuilt(p, j):
                dve.wait_ge(xres_ld[p.par], (p.pos() + 1) * 16)
                if not (isinstance(p.pair, int) and p.off < 1):
                    dve.wait_ge(out_st[j], p.nth(16, 0))
                V.tensor_scalar(o[:, j], x_res[:, p.par, j], st_keep[p.par][:, 0, j:j + 1],
                                st_keep[p.par][:, 1, j:j + 1], ALU.subtract, ALU.mult).then_inc(xn_again, 1)

            def y_added(p, j):
                dve.wait_ge(y_mm, p.nth(J, j + 1))
                dve.wait_ge(xn_again, p.nth(J, j + 1))
                V.tensor_tensor(o[:, j], y_ps, o[:, j], ALU.add).then_inc(y_add, 1)

            def step(t, main=True, prev=True, nxt=True, begun=False):
                p, n = t + -1, t + 1
                if nxt and not begun:
                    stats(n)
                if prev:
                    doubled(p, LEVELS)
                if main and not begun:
                    kq_rows(t)
                if prev:
                    inverse_done(p)
                    t_low(p)
                if main and not begun:
                    v_rows(t, 0)
                if nxt:
                    carry_over(n)
                if prev:
                    xn_rebuilt(p, 0)
                if nxt and not begun:
                    normalise(n)
                if prev:
                    kp_low(p)
                if main and not begun:
                    masked(t)
                    v_rows(t, 1)
                if prev:
                    u_low(p, 0)
                if main and not begun:
                    coupled(t, 1)
                if main:
                    gate_mix(t, 1)
                if nxt:
                    first_column(n)
                if main:
                    doubled(t, 1)
                if prev:
                    s_low(p, 0)
                    y_added(p, 0)
                if main:
                    squared(t, 0)
                    coupled(t, 2)
                    doubled(t, 2)
                if prev:
                    xn_rebuilt(p, 1)
                    u_low(p, 1)
                if main:
                    squared(t, 1)
                    coupled(t, 3)
                    doubled(t, 3)
                if prev:
                    s_low(p, 1)
                    y_added(p, 1)
                if main:
                    coupled(t, 4)
                if nxt:
                    key_mix(n, 0)
                if main:
                    doubled(t, 4)
                if nxt:
                    key_halves(n, 0)
                if main:
                    coupled(t, 5)
                if nxt:
                    key_mix(n, 1)
                if main:
                    doubled(t, 5)
                if nxt:
                    key_halves(n, 1)
                if main:
                    gated_mix(t, 0)
                    coupled(t, 6)
                if nxt:
                    gate_mix(n, 0)
                if main:
                    gated_mix(t, 1)

            first = Tile(0, 0)
            stats(first)
            dve.wait_ge(cols_ld, 16)
            V.tensor_copy(beta_b, cols[:, 1].unsqueeze(2).to_broadcast([P, CC, P])).then_inc(beta_bc, 1)
            dve.wait_ge(ident_done, 1)
            V.tensor_scalar(lastT, ident, 1.0, None, ALU.add).then_inc(pick_sum, 1)
            normalise(first)
            first_column(first)
            weight_low(0)
            stats(first + 1)
            xn_low(first)
            dve.wait_ge(pick_first, 1)
            dve.wait_ge(pick_sum, 1)
            V.tensor_tensor(pick[:, :, 1], lastT.unsqueeze(1).to_broadcast([P, LEVELS, C]), pick[:, :, 0],
                            ALU.subtract)
            weight_low(1)
            dve.wait_ge(bias_ld, 32)
            for n, bias, ps in ((0, bias_kq, b_ps[:, 0:KQ]), (1, bias_v, a_ps)):
                dve.wait_ge(bias_mm, n + 1)
                V.tensor_tensor(bias, ps, bias, ALU.add).then_inc(bias_add, 1)
            dve.wait_ge(bias_add, 2)
            V.tensor_scalar(bias_v, bias_v, LR, None, ALU.mult)
            kq_rows(first)
            v_rows(first, 0)
            key_mix(first, 0)
            key_halves(first, 0)
            masked(first)
            v_rows(first, 1)
            key_mix(first, 1)
            key_halves(first, 1)
            normalise(first + 1)
            coupled(first, 1)
            gate_mix(first, 0)
            step(first, prev=False, begun=True)
            for t in range(1, FIRST):
                step(Tile(0, t))
            with dve.Fori(0, PAIRS) as i:
                for b in range(2):
                    step(Tile(i, FIRST + b))
            step(Tile(0, NT - 1), nxt=False)
            step(Tile(0, NT), main=False, nxt=False)

        @block.tensor
        def _(pe):
            def mm(out_, lhsT, rhs, start, stop):
                return nc.tensor.matmul(out_, lhsT, rhs, start=start, stop=stop)

            def split_mm(out_, w, m, start, stop):
                mm(out_, w[1], m[0], start, False)
                mm(out_, w[0], m[0], False, False)
                return mm(out_, w[0], m[1], False, stop)

            def cut(pair, *at_):
                return pair[0][at_], pair[1][at_]

            ALL = slice(None)

            def bias_through_beta(n):
                pe.wait_ge(beta_bc, 1)
                pe.wait_ge(w_ld[n], 32)
                out_ = (b_ps[:, 0:KQ], a_ps)[n]
                for c in range(CC):
                    last = mm(out_, beta_b[:, c], WEIGHTS[n][1][c // HC][:, c % HC], c == 0, c == CC - 1)
                last.then_inc(bias_mm, 1)

            def xn_transposes(n, j):
                pe.wait_ge(xn_done, n.nth(1, 1))
                if isinstance(n.pair, int) and n.off == 0:
                    pe.wait_ge(ident_done, 1)
                elif j == 0:
                    pe.wait_ge(v_ev, (n + -1).nth(J, 2))
                else:
                    pe.wait_ge(relu_ev, (n + -1).nth(2, 1))
                f = bank(n + -1, f"xt{j}")
                for c in range(CC):
                    last = nc.tensor.transpose(f[:, c * C:(c + 1) * C], xn[:, j, c * P:(c + 1) * P], ident)
                last.then_inc(xt_mm, 1)

            def kq(t):
                pe.wait_ge(xnT_lo, t.nth(1, 1))
                if not (isinstance(t.pair, int) and t.off < 1):
                    pe.wait_ge(mix_ev, (t + -1).nth(J, 1))
                else:
                    pe.wait_ge(w_lo_dve, 1)
                    pe.wait_ge(xt_ev, t.nth(J, 2))
                f = bank(t, "kq")
                for c in range(CC):
                    last = split_mm(f[:, 0:TT], cut(wkq, ALL, c), cut(xnT, ALL, c), c == 0, c == CC - 1)
                last.then_inc(kq_mm, 1)

            def kq_by_rows(t):
                pe.wait_ge(kq_copied, t.nth(1, 1))
                f = bank(t, "kq")
                for j in range(J):
                    last = nc.tensor.transpose(f[:, TT + j * C:TT + (j + 1) * C], kqT32[:, j * C:(j + 1) * C], ident)
                last.then_inc(kq_back, 1)

            def v_half(t, j, h):
                if t.off == 0:
                    pe.wait_ge(w_lo_dve, 2)
                if h == 0:
                    if j == 1:
                        pe.wait_ge(kq_ev, t.nth(1, 1))
                    elif not (isinstance(t.pair, int) and t.off < 1):
                        pe.wait_ge(mix_ev, (t + -1).nth(J, 2))
                f = bank(t, f"v{j}")
                for c in (2 * h, 2 * h + 1):
                    last = split_mm(f, cut(xnT, ALL, c, slice(j * C, (j + 1) * C)), cut(wv, ALL, c),
                                    c == 0, c == CC - 1)
                if h:
                    last.then_inc(v_mm, 1)

            def k_half(t, m, h):
                if h == 0:
                    if m == 0:
                        pe.wait_ge(xk_lo, t.nth(2, 2))
                        if t.off == 0:
                            pe.wait_ge(w_lo_pool, 1)
                        pe.wait_ge(v_ev, t.nth(J, 1))
                    elif t.off < NT - 1:
                        pe.wait_ge(xt_ev, (t + 1).nth(J, 1))
                    else:
                        pe.wait_ge(v_ev, t.nth(J, 2))
                f = bank(t, f"k{m}")
                d = 2 * m + h
                for c in range(CC):
                    last = split_mm(f[:, h * TT:(h + 1) * TT], cut(wfk, ALL, c, slice(d * P, (d + 1) * P)),
                                    cut(xkT, ALL, c), c == 0, c == CC - 1)
                if h:
                    last.then_inc(k_mm, 1)

            def r_half(t, j, h):
                if h == 0:
                    if j == 0:
                        pe.wait_ge(xr_lo, t.nth(2, 2))
                        if t.off == 0:
                            pe.wait_ge(w_lo_pool, 2)
                        if t.off < NT - 1:
                            pe.wait_ge(xt_ev, (t + 1).nth(J, 2))
                        else:
                            pe.wait_ge(relu_ev, t.nth(2, 1))
                    else:
                        pe.wait_ge(relu_ev, t.nth(2, 2))
                f = bank(t, f"r{j}")
                for c in (2 * h, 2 * h + 1):
                    last = split_mm(f, cut(xrT, ALL, c, slice(j * C, (j + 1) * C)), cut(wr, ALL, c),
                                    c == 0, c == CC - 1)
                if h:
                    last.then_inc(r_mm, 1)

            def kv_half(t, j, h):
                if h == 0:
                    pe.wait_ge(r_ev, t.nth(J, j + 1))
                    pe.wait_ge(act_lo, t.nth(2, 2))
                    if t.off == 0:
                        pe.wait_ge(w_lo_pool, 3)
                f = bank(t, f"mix{j}")
                for c in (2 * h, 2 * h + 1):
                    last = split_mm(f, cut(actT, ALL, c, slice(j * C, (j + 1) * C)), cut(wfv, ALL, c),
                                    c == 0, c == CC - 1)
                if h:
                    last.then_inc(kv_mm, 1)

            def kq_transposes(t, j):
                if j == 0:
                    pe.wait_ge(kn_lo, t.nth(1, 1))
                    pe.wait_ge(qn_lo, t.nth(1, 1))
                    if not (isinstance(t.pair, int) and t.off < 1):
                        pe.wait_ge(t_done, t.nth(1, 0))
                elif not (isinstance(t.pair, int) and t.off < 1):
                    pe.wait_ge(x_up, t.nth(LEVELS, 0))
                dst = (b_ps, a_ps)[j]
                rows = kn[t.par][:, j].bitcast(F32)
                sources = [rows[:, DS:3 * DS], rows[:, 3 * DS:5 * DS]]
                sources.insert((0, 2)[t.par], qn[:, j].bitcast(F32))
                for k, source in enumerate(sources):
                    last = nc.tensor.transpose(dst[:, k * C:(k + 1) * C], source, ident)
                last.then_inc(kqT_mm, 1)

            def products(t):
                pe.wait_ge(kqT_ev, t.nth(J, 2))
                for j in range(J):
                    both = kqT[:, j, KQT_KQ[t.par]]
                    dst = a_ps[:, 2 * j * C:2 * (j + 1) * C].rearrange("p (k q) -> p k q", k=2)
                    mm(dst, kqT[:, j, 1], both, True, False)
                    last = mm(dst, kqT[:, j, 2], both, False, True)
                last.then_inc(g_mm, 1)

            def couple_blocks(t, i):
                pe.wait_ge(picked, t.nth(LEVELS, i))
                if i == 1:
                    pe.wait_ge(z_done, t.nth(1, 1))
                    if not (isinstance(t.pair, int) and t.off < 1):
                        pe.wait_ge(kp_lo, t.nth(1, 0))
                mm(a_ps[:, 0:C], z, ypick[:, 0], True, True).then_inc(ox_mm, 1)
                nc.tensor.transpose(b_ps[:, 0:C], ypick[:, 1], ident).then_inc(xT_mm, 1)

            def double_blocks(t, i):
                pe.wait_ge(ox_ev, t.nth(LEVELS, i))
                pe.wait_ge(xT_ev, t.nth(LEVELS, i))
                mm(a_ps[:, C:2 * C], lastT, ox, True, True).then_inc(xox_mm, 1)

            def inverse_transposed(p):
                pe.wait_ge(x_up, p.nth(LEVELS, LEVELS))
                nc.tensor.transpose(b_ps[:, 0:C], y, ident).then_inc(yT_mm, 1)

            def tk(p):
                pe.wait_ge(t_lo, p.nth(1, 1))
                if p.off < NT - 1:
                    pe.wait_ge(kqT_ev, (p + 1).nth(J, 1))
                for j in range(J):
                    rows = kn[p.par][:, j]
                    last = split_mm(b_ps[:, j * C:(j + 1) * C], (rows[:, 0:2 * DS], rows[:, 2 * DS:4 * DS]),
                                    cut(tT, ALL, j), True, True)
                last.then_inc(kp_mm, 1)

            def u_and_qs(p, j):
                if j == 0:
                    pe.wait_ge(kp_lo, p.nth(1, 1))
                    pe.wait_ge(v_lo, p.nth(J, 2))
                if j or not (isinstance(p.pair, int) and p.off < 1):
                    pe.wait_ge(u_lo, p.nth(J, j))
                    pe.wait_ge(sc_lo, p.nth(J, j))
                split_mm(u_ps, cut(tT, ALL, j), cut(v[p.par], ALL, j), True, False)
                mm(u_ps, kp[:, j], s_hi[p.par], False, False)
                mm(u_ps, kp[:, j], s_lo[p.par], False, True).then_inc(u_mm, 1)
                if j or not (isinstance(p.pair, int) and p.off < 1):
                    pe.wait_ge(y_add, p.nth(J, j))
                mm(y_ps, kqT[:, j, KQT_Q[p.par]], s_hi[p.par], True, False)
                mm(y_ps, kqT[:, j, KQT_Q[p.par]], s_lo[p.par], False, False)

            def s_and_y(p, j):
                pe.wait_ge(u_lo, p.nth(J, j + 1))
                rows = kn[p.par][:, j]
                for w, m in ((0, 0), (1, 0), (0, 1)):
                    last = nc.tensor.matmul(s_ps[p.par], rows[:, 2 * w * DS:2 * (w + 1) * DS], u[m],
                                            start=False, stop=False, skip_group_check=True)
                last.then_inc(s_mm, 1)
                pe.wait_ge(at_lo, p.nth(1, 1))
                split_mm(y_ps, cut(at[p.par], ALL, j), u, False, True).then_inc(y_mm, 1)

            def step(t, main=True, prev=True, nxt=True):
                p, n = t + -1, t + 1
                if main:
                    kq(t)
                if prev:
                    double_blocks(p, LEVELS)
                if main:
                    v_half(t, 0, 0)
                    kq_by_rows(t)
                if prev:
                    inverse_transposed(p)
                if main:
                    v_half(t, 0, 1)
                    v_half(t, 1, 0)
                    kq_transposes(t, 0)
                    kq_transposes(t, 1)
                    v_half(t, 1, 1)
                if prev:
                    tk(p)
                if main:
                    products(t)
                    k_half(t, 0, 0)
                if prev:
                    u_and_qs(p, 0)
                if main:
                    couple_blocks(t, 1)
                    k_half(t, 0, 1)
                if nxt:
                    xn_transposes(n, 0)
                if prev:
                    s_and_y(p, 0)
                if main:
                    double_blocks(t, 1)
                    k_half(t, 1, 0)
                    couple_blocks(t, 2)
                if nxt:
                    xn_transposes(n, 1)
                if main:
                    k_half(t, 1, 1)
                    double_blocks(t, 2)
                if prev:
                    u_and_qs(p, 1)
                if main:
                    couple_blocks(t, 3)
                    r_half(t, 0, 0)
                if prev:
                    s_and_y(p, 1)
                if main:
                    double_blocks(t, 3)
                    r_half(t, 0, 1)
                    couple_blocks(t, 4)
                    r_half(t, 1, 0)
                    double_blocks(t, 4)
                    r_half(t, 1, 1)
                    couple_blocks(t, 5)
                    kv_half(t, 0, 0)
                    double_blocks(t, 5)
                    kv_half(t, 0, 1)
                    couple_blocks(t, 6)
                    kv_half(t, 1, 0)
                    kv_half(t, 1, 1)

            pe.wait_ge(dve_zero, 1)
            for i in range(2):
                nc.tensor.matmul(s_ps[i], s_hi[i][:, 0:P], s_hi[i], start=True, stop=False,
                                 skip_group_check=True)
            bias_through_beta(0)
            for j in range(J):
                xn_transposes(Tile(0, 0), j)
            bias_through_beta(1)
            step(Tile(0, 0), prev=False)
            for t in range(1, FIRST):
                step(Tile(0, t))
            with pe.Fori(0, PAIRS) as i:
                for b in range(2):
                    step(Tile(i, FIRST + b))
            step(Tile(0, NT - 1), nxt=False)
            step(Tile(0, NT), main=False, nxt=False)


def kernel(L0_attn_x, L0_attn_Wk, L0_attn_bk, L0_attn_Wv, L0_attn_bv, L0_attn_Wq, L0_attn_bq, L0_attn_gamma,
           L0_attn_beta, L0_ffn_W_r, L0_ffn_W_k, L0_ffn_W_v, L0_ffn_mu_r, L0_ffn_mu_k):
    import numpy as np
    import concourse.bacc as bacc
    from concourse.bass_utils import run_bass_kernel_spmd

    def by_channel(a):
        return np.transpose(np.reshape(a, (-1, 128)))

    arrays = {
        "x": L0_attn_x, "Wkq_t": np.transpose(np.concatenate([L0_attn_Wk, L0_attn_Wq])),
        "bkq": np.concatenate([L0_attn_bk, L0_attn_bq]), "Wv_t": np.transpose(L0_attn_Wv), "bv": L0_attn_bv,
        "columns": np.stack([by_channel(a) for a in (L0_attn_gamma, L0_attn_beta, L0_ffn_mu_r, L0_ffn_mu_k)],
                            axis=1),
        "Wr_t": np.transpose(L0_ffn_W_r), "Wfk_t": np.transpose(L0_ffn_W_k), "Wfv_t": np.transpose(L0_ffn_W_v),
    }
    arrays = {name: np.ascontiguousarray(a) for name, a in arrays.items()}
    nc = bacc.Bacc("TRN2", target_bir_lowering=False, num_devices=1)
    args = [nc.dram_tensor(name, a.shape, mybir.dt.from_np(a.dtype), kind="ExternalInput").ap()
            for name, a in arrays.items()]
    out = nc.dram_tensor("out", arrays["x"].shape, F32, kind="ExternalOutput").ap()
    build(nc, *args, out)
    result = run_bass_kernel_spmd(nc, [arrays], core_ids=[0])
    return result.results[0]["out"]
```
